# Optimizing a Trainium2 kernel written in Bass

```python
import numpy as np
import jax
import jax.numpy as jnp

def _softmax(x, axis=-1):
    return jax.nn.softmax(x, axis=axis)

def _gelu(x):
    return jax.nn.gelu(x, approximate=True)

def _silu(x):
    return jax.nn.silu(x)

def _sigmoid(x):
    return jax.nn.sigmoid(x)

def _layernorm(x, axis=-1, eps=1e-05):
    m = jnp.mean(x, axis=axis, keepdims=True)
    v = jnp.var(x, axis=axis, keepdims=True)
    return (x - m) / jnp.sqrt(v + eps)

def _scatter_add(tgt, idx, src, axis=0):
    return tgt.at[idx].add(src)

def _segment_sum(src, seg, n):
    return jax.ops.segment_sum(src, seg, n)
kernel_name = 'mk_conv_preact_d2_conv_nchw256_r4_c5e8cd'

def setup_inputs(seed: int=0):
    np.random.seed(seed)
    _w = jnp.asarray

    def _rec_inputs():
        import jax
        import jax.numpy as jnp
        _gk = jax.random.key(seed)
        x = -0.0002023 + 1 * jax.random.normal(jax.random.fold_in(_gk, 1), (32, 64, 28, 28), jnp.float32)
        return x
    x = _rec_inputs()

    def _L0_conv_setup():
        import jax, jax.numpy as jnp
        import numpy as np
        PARALLEL = 4
        EPS = 1e-05

        @jax.custom_vjp
        def binarize(x):
            return jnp.sign(x)

        def _bin_fwd(x):
            return (jnp.sign(x), x)

        def _bin_bwd(x, g):
            return (g * (jnp.abs(x) <= 1.0).astype(g.dtype),)
        binarize.defvjp(_bin_fwd, _bin_bwd)

        def bconv3x3(x, w, groups, stride=1):
            return jax.lax.conv_general_dilated(binarize(x), binarize(w), window_strides=(stride, stride), padding=[(1, 1), (1, 1)], feature_group_count=groups, dimension_numbers=('NCHW', 'OIHW', 'NCHW'))

        def batchnorm(x, scale, bias, mean, var):
            inv = scale * jax.lax.rsqrt(var + EPS)
            return x * inv[None, :, None, None] + (bias - mean * inv)[None, :, None, None]
        key = jax.random.key(seed)
        ks = jax.random.split(key, 12)
        f32 = jnp.float32
        return {'x': jax.random.normal(ks[0], (32, 64, 28, 28), dtype=f32), 'w1': jax.random.normal(ks[1], (256, 64, 3, 3), dtype=f32), 'bn1_scale': jax.random.uniform(ks[2], (256,), dtype=f32), 'bn1_bias': jax.random.normal(ks[3], (256,), dtype=f32), 'bn1_mean': jax.random.normal(ks[4], (256,), dtype=f32), 'bn1_var': jax.random.uniform(ks[5], (256,), dtype=f32), 'w2': jax.random.normal(ks[6], (256, 64, 3, 3), dtype=f32), 'bn2_scale': jax.random.uniform(ks[7], (256,), dtype=f32), 'bn2_bias': jax.random.normal(ks[8], (256,), dtype=f32), 'bn2_mean': jax.random.normal(ks[9], (256,), dtype=f32), 'bn2_var': jax.random.uniform(ks[10], (256,), dtype=f32), 'lambdas': jax.random.uniform(ks[11], (4,), dtype=f32)}
    _L0_conv_all = _L0_conv_setup()
    _L0_conv_in = {k: v for k, v in _L0_conv_all.items() if k in ('w1', 'bn1_scale', 'bn1_bias', 'bn1_mean', 'bn1_var', 'w2', 'bn2_scale', 'bn2_bias', 'bn2_mean', 'bn2_var', 'lambdas')}
    del _L0_conv_all

    def _L1_conv_setup():
        import jax, jax.numpy as jnp
        import numpy as np
        SELECTED_CLASSES = 5
        EPS = 1e-05
        key = jax.random.key(seed)
        k1, k2, k3 = jax.random.split(key, 3)
        x = jax.random.normal(k1, (8, 64, 32, 32), dtype=jnp.float32)
        masks = jax.random.uniform(k2, (8, 128, 128), dtype=jnp.float32)
        conv_w = jax.random.normal(k3, (1, 3, 7, 7), dtype=jnp.float32) * 0.05
        in_gamma = jnp.ones((64,), dtype=jnp.float32)
        in_beta = jnp.zeros((64,), dtype=jnp.float32)
        return {'x': x, 'masks': masks, 'conv_w': conv_w, 'in_gamma': in_gamma, 'in_beta': in_beta}
    _L1_conv_all = _L1_conv_setup()
    _L1_conv_in = {k: v for k, v in _L1_conv_all.items() if k in ('masks', 'conv_w', 'in_gamma', 'in_beta')}
    del _L1_conv_all
    return {'x': x, 'L0_conv_w1': _L0_conv_in['w1'], 'L0_conv_bn1_scale': _L0_conv_in['bn1_scale'], 'L0_conv_bn1_bias': _L0_conv_in['bn1_bias'], 'L0_conv_bn1_mean': _L0_conv_in['bn1_mean'], 'L0_conv_bn1_var': _L0_conv_in['bn1_var'], 'L0_conv_w2': _L0_conv_in['w2'], 'L0_conv_bn2_scale': _L0_conv_in['bn2_scale'], 'L0_conv_bn2_bias': _L0_conv_in['bn2_bias'], 'L0_conv_bn2_mean': _L0_conv_in['bn2_mean'], 'L0_conv_bn2_var': _L0_conv_in['bn2_var'], 'L0_conv_lambdas': _L0_conv_in['lambdas'], 'L1_conv_masks': _L1_conv_in['masks'], 'L1_conv_conv_w': _L1_conv_in['conv_w'], 'L1_conv_in_gamma': _L1_conv_in['in_gamma'], 'L1_conv_in_beta': _L1_conv_in['in_beta']}

def reference(x, L0_conv_w1, L0_conv_bn1_scale, L0_conv_bn1_bias, L0_conv_bn1_mean, L0_conv_bn1_var, L0_conv_w2, L0_conv_bn2_scale, L0_conv_bn2_bias, L0_conv_bn2_mean, L0_conv_bn2_var, L0_conv_lambdas, L1_conv_masks, L1_conv_conv_w, L1_conv_in_gamma, L1_conv_in_beta):
    import jax
    import jax.numpy as jnp

    def _L0_conv_ref(x, w1, bn1_scale, bn1_bias, bn1_mean, bn1_var, w2, bn2_scale, bn2_bias, bn2_mean, bn2_var, lambdas):
        import jax, jax.numpy as jnp
        import numpy as np
        PARALLEL = 4
        EPS = 1e-05

        @jax.custom_vjp
        def binarize(x):
            return jnp.sign(x)

        def _bin_fwd(x):
            return (jnp.sign(x), x)

        def _bin_bwd(x, g):
            return (g * (jnp.abs(x) <= 1.0).astype(g.dtype),)
        binarize.defvjp(_bin_fwd, _bin_bwd)

        def bconv3x3(x, w, groups, stride=1):
            return jax.lax.conv_general_dilated(binarize(x), binarize(w), window_strides=(stride, stride), padding=[(1, 1), (1, 1)], feature_group_count=groups, dimension_numbers=('NCHW', 'OIHW', 'NCHW'))

        def batchnorm(x, scale, bias, mean, var):
            inv = scale * jax.lax.rsqrt(var + EPS)
            return x * inv[None, :, None, None] + (bias - mean * inv)[None, :, None, None]
        identity = x
        xr = jnp.tile(x, (1, PARALLEL, 1, 1))
        out = bconv3x3(xr, w1, groups=PARALLEL, stride=1)
        out = jax.nn.relu(batchnorm(out, bn1_scale, bn1_bias, bn1_mean, bn1_var))
        out = bconv3x3(out, w2, groups=PARALLEL, stride=1)
        out = batchnorm(out, bn2_scale, bn2_bias, bn2_mean, bn2_var)
        B, C, H, W = out.shape
        planes = C // PARALLEL
        out = out * jnp.repeat(lambdas, planes)[None, :, None, None]
        out = out.reshape(B, PARALLEL, planes, H, W).sum(axis=1)
        return jax.nn.relu(out + identity)

    def _L1_conv_ref(x, masks, conv_w, in_gamma, in_beta):
        import jax, jax.numpy as jnp
        import numpy as np
        SELECTED_CLASSES = 5
        EPS = 1e-05
        B, C, H, W = x.shape
        m = masks[:, None, :, :] if masks.ndim == 3 else masks
        m = jax.image.resize(m, (B, 1, H, H), method='bilinear')
        mid = x * m
        avg_out = jnp.mean(mid, axis=1, keepdims=True)
        max_out = jnp.max(mid, axis=1, keepdims=True)
        atten = jnp.concatenate([avg_out, max_out, m], axis=1)
        atten = jax.lax.conv_general_dilated(atten, conv_w, window_strides=(1, 1), padding=[(3, 3), (3, 3)], dimension_numbers=('NCHW', 'OIHW', 'NCHW'))
        atten = jax.nn.sigmoid(atten)
        out = mid * atten
        mu = jnp.mean(out, axis=(2, 3), keepdims=True)
        var = jnp.var(out, axis=(2, 3), keepdims=True)
        rn = (out - mu) * jax.lax.rsqrt(var + EPS)
        rn = rn * in_gamma[None, :, None, None] + in_beta[None, :, None, None]
        return jax.nn.relu(SELECTED_CLASSES * rn)

    def _gn(v, G=32, eps=1e-05):
        B_, C_, H_, W_ = v.shape
        g = v.reshape(B_, G, C_ // G, H_, W_)
        m = jnp.mean(g, axis=(2, 3, 4), keepdims=True)
        s = jnp.var(g, axis=(2, 3, 4), keepdims=True)
        return ((g - m) / jnp.sqrt(s + eps)).reshape(v.shape)

    def _ln_c(v, eps=1e-06):
        m = jnp.mean(v, axis=1, keepdims=True)
        s = jnp.var(v, axis=1, keepdims=True)
        return (v - m) / jnp.sqrt(s + eps)

    def _ln_t(v, eps=1e-05):
        m = jnp.mean(v, axis=-1, keepdims=True)
        s = jnp.var(v, axis=-1, keepdims=True)
        return (v - m) / jnp.sqrt(s + eps)

    def _to_tokens(v):
        B_, C_, H_, W_ = v.shape
        return v.reshape(B_, C_, H_ * W_).transpose(0, 2, 1)

    def _from_tokens(t, like):
        B_, C_, H_, W_ = like.shape
        return t.transpose(0, 2, 1).reshape(B_, C_, H_, W_)
    x = x + _L0_conv_ref(_gn(x), L0_conv_w1, L0_conv_bn1_scale, L0_conv_bn1_bias, L0_conv_bn1_mean, L0_conv_bn1_var, L0_conv_w2, L0_conv_bn2_scale, L0_conv_bn2_bias, L0_conv_bn2_mean, L0_conv_bn2_var, L0_conv_lambdas)
    x = x + _L1_conv_ref(_gn(x), L1_conv_masks, L1_conv_conv_w, L1_conv_in_gamma, L1_conv_in_beta)
    return x

_drawn_inputs = setup_inputs


def setup_inputs(seed=0):
    import zlib

    import numpy as np

    out = dict(_drawn_inputs(seed))
    spreads = {'L1_conv_in_gamma': (1.0, 0.2), 'L1_conv_in_beta': (0.0, 0.627)}
    factors = {'L1_conv_masks': 3.774}
    for name, (base, spread) in spreads.items():
        noise = np.random.default_rng([zlib.crc32(name.encode()), seed]).standard_normal(out[name].shape)
        drawn = base * np.exp(spread * noise) if base else spread * noise
        out[name] = jnp.asarray(drawn.astype(out[name].dtype))
    for name, factor in factors.items():
        out[name] = (out[name] * factor).astype(out[name].dtype)
    return out
```

```python
from contextlib import ExitStack

import numpy as np

import concourse.bass as bass
from concourse import mybir

ALU = mybir.AluOpType
ACT = mybir.ActivationFunctionType
AX_X = mybir.AxisListType.X
F32 = mybir.dt.float32
BF16 = mybir.dt.bfloat16
F16 = mybir.dt.float16

P = 128
B, C, H, W = 32, 64, 28, 28
HW = H * W
HALF = HW // 2
RH = H // 2
NT = B // 2
G = 4
PW = W + 2
PAD = (H + 2) * PW
PADX = PAD + 32
KS = 5
CH = 4
CP = CH * W
NJ = H // CH
MB, MH, MW = 8, 128, 128
KW = 7
NCH = 3
EPS = 1e-5
ROUND = 1.5 * 2.0 ** 23
SHIFT = 2.0 ** 11
SELECTED = 5.0

K_ID = 0
K_MEAN = K_ID + P
K_PAIR = K_MEAN + 2
K_FOLD = K_PAIR + P
K_SEL = K_FOLD + P
K_RH = K_SEL + 64
K_RW = K_RH + H
K_SCALE = K_RW + CH * CP
K_N = K_SCALE + 1
Q_SCALE, Q_BIAS, Q_MEAN, Q_VAR, Q_LAM, Q_GAMMA, Q_BETA, Q_N = 0, 4, 8, 12, 16, 18, 19, 20

LAST_SKEW = 9
STEPS = NT + LAST_SKEW + 1


class Pair:

    def __init__(self, h, off):
        self.known = isinstance(h, int)
        self.t = h * 2 + off if off else h * 2
        self.half = h + off // 2 if off // 2 else h
        self.par = off % 2

    def runs(self):
        return not self.known or 0 <= self.t < NT


def wait(eng, sem, count):
    if isinstance(count, int) and count <= 0:
        return
    eng.wait_ge(sem, count)


UNITS = ["c1_0", "c1_1", "y", "c1_2", "c1_3", "c2_0", "c2_1"]
SKEW = {"c1": 2, "y": 4, "c2": 3}


def unit_slot(par, name):
    return (len(UNITS) * par + UNITS.index(name)) % 3


def unit_before(step_known, k, par, name):
    back, pos = 0, UNITS.index(name)
    slot = unit_slot(par, name)
    while True:
        pos -= 1
        if pos < 0:
            pos, back = len(UNITS) - 1, back + 1
        if step_known and k - back < 0:
            return None
        other = UNITS[pos]
        if unit_slot((par - back) % 2, other) != slot:
            continue
        if step_known and not 0 <= k - back - SKEW[other.split("_")[0]] < NT:
            continue
        return back, other


def run_steps(eng, first_loop, step):
    for k in range(first_loop):
        step(k // 2, k % 2)
    with eng.Fori(first_loop // 2, NT // 2) as h:
        step(h, 0)
        step(h, 1)
    for k in range(NT, STEPS):
        step(k // 2, k % 2)


def build(nc, x, w1, w2, par, masks, att_w, cst, sel, out):
    x_v = x.rearrange("(t i) c h w -> t (i c) (h w)", i=2)
    out_v = out.rearrange("(t i) c h w -> t (i c) (h w)", i=2)
    m_dram = nc.dram_tensor("mask_rows", (B, HW), F32, kind="Internal").ap()
    a_dram = nc.dram_tensor("attention_rows", (B, HW), F32, kind="Internal").ap()
    m_group = m_dram.rearrange("(g b) (j n) -> g j b n", b=4, n=CP)
    a_group = a_dram.rearrange("(g b) (j n) -> g j b n", b=4, n=CP)

    ctx = ExitStack()
    with ctx:
        def sb(name, shape, dt):
            return ctx.enter_context(nc.sbuf_tensor(name, shape, dt))

        def sem(name):
            return ctx.enter_context(nc.semaphore(name))

        X = sb("X", [P, NT, HW], F32)
        U = sb("U", [P, 2, PADX], BF16)
        R = sb("R", [P, 2, 2, 2, PAD], BF16)
        relu = sb("relu", [P, 2, HW], BF16)
        S2 = sb("S2", [P, 2, 2, 2, PAD], BF16)
        RD = sb("RD", [P, 2, 2, 2, HW], F16)
        acc0 = sb("acc0", [P, 2, HW], F32)
        ysum = sb("ysum", [P, HW], F32)
        mask_b = sb("mask_b", [P, 2, HW], F32)
        u = sb("u", [P, 2, HW], F32)
        diag = sb("diag", [P, 2, P + 2], F32)
        att_b = sb("att_b", [P, 2, HW], F32)
        o = sb("o", [P, 2, HW], F32)
        fin = sb("fin", [P, 2, HW], F32)
        red = sb("red", [CP, NCH, NJ + 2, 4], F32)
        att_s = sb("att_s", [4 * NJ, CP], F32)
        att_m = sb("att_m", [4 * NJ, CP], F32)
        mask_r = sb("mask_r", [4 * NJ, CP], F32)
        bnst = sb("bnst", [P, 3, 2, 6], F32)
        mv1 = sb("mv1", [P, 2, 2], F32)
        mv2 = sb("mv2", [P, 2, 2], F32)
        mv3 = sb("mv3", [P, 2, 2], F32)
        nm1 = sb("nm1", [P, 2], F32)
        ve1 = sb("ve1", [P, 2], F32)
        r1 = sb("r1", [P, 2], F32)
        b1 = sb("b1", [P, 2], F32)
        dm = sb("dm", [P, 2], F32)
        nm2 = sb("nm2", [P, NT], F32)
        ve2 = sb("ve2", [P, 2], F32)
        r2p = sb("r2p", [P, 2], F32)
        r2 = sb("r2", [P, NT], F32)
        ve3 = sb("ve3", [P, 2], F32)
        r3 = sb("r3", [P, 2], F32)
        sc3 = sb("sc3", [P, 2], F32)
        bi3 = sb("bi3", [P, 2], F32)
        tmp = sb("tmp", [P, 4], F32)
        w1s = sb("w1s", [P, KS, 2 * P], BF16)
        w2s = sb("w2s", [P, 2, 9, 64], BF16)
        w2t = sb("w2t", [P, 2, 9, 64], BF16)
        wa = sb("wa", [P, 2, 3, 64], BF16)
        cs = sb("cs", [P, K_N], F32)
        selz = sb("selz", [CH * KW, W, CP], F32)
        atw = sb("atw", [CH * KW, NCH * 3 * CH], F32)
        band = sb("band", [CP, NCH * 3 * CH, W], F32)
        prm = sb("prm", [P, Q_N], F32)
        pv = sb("pv", [P, 4], F32)
        rs = sb("rs", [P, 4], F32)
        inv = sb("inv", [P, 4], F32)
        shf = sb("shf", [P, 4], F32)
        alpha = sb("alpha", [P, 2], F32)
        rest = sb("rest", [P, 2, 2], F32)
        part = sb("part", [P, 3, 2], BF16)
        kap = sb("kap", [P, 2], F32)
        kaps = sb("kaps", [P, 1], F32)
        beta = sb("beta", [P, 1], F32)
        g5 = sb("g5", [P, 2], F32)
        mhalf = sb("mhalf", [P, 4], F32)
        mfull = sb("mfull", [MH, MB, MW], F32)
        mh = sb("mh", [MW, MB, H], F32)
        mhw = sb("mhw", [CP, MB + 2, NJ], F32)
        mlo = sb("mlo", [CP, MB, NJ], F32)
        mT = sb("mT", [CP, B, NJ], F32)
        mR = sb("mR", [CP, 2, CP], F32)
        w1f = o[:, :, :].rearrange("p a n -> p (a n)")[:, 0:KS * 2 * P]
        w2f = fin[:, :, :].rearrange("p a n -> p (a n)")[:, 0:2 * 9 * 64]

        big = [ctx.enter_context(nc.psum_tensor(f"big{i}", [P, 2, 512], F32)) for i in range(3)]
        small = [ctx.enter_context(nc.psum_tensor(f"small{i}", [P, 512], F32)) for i in range(2)]

        x_in = [sem(f"x_in{i}") for i in range(2)]
        w1_in, w2_in, par_in, cst_in, mask_in, att_in = (
            sem(n) for n in ("w1_in", "w2_in", "par_in", "cst_in", "mask_in", "att_in"))
        w1_signs, w2_signs, w2_ready = sem("w1_signs"), sem("w2_signs"), sem("w2_ready")
        cleared, prep, prep_pow, bn1_ready = sem("cleared"), sem("prep"), sem("prep_pow"), sem("bn1_ready")
        mix_ready, beta_ready, beta_sum = sem("mix_ready"), sem("beta_ready"), sem("beta_sum")
        mask_h, mask_hs, mask_hw, mask_mix, mask_turned, mask_rows = (
            sem(n) for n in ("mask_h", "mask_hs", "mask_hw", "mask_mix", "mask_turned", "mask_rows"))
        mask_stored, band_made, band_ready, half_ready = (
            sem(n) for n in ("mask_stored", "band_made", "band_ready", "half_ready"))
        stats1, stats2, stats3 = sem("stats1"), sem("stats2"), sem("stats3")
        local1, local2 = sem("local1"), sem("local2")
        group1, group2 = sem("group1"), sem("group2")
        mean1, mean2 = sem("mean1"), sem("mean2")
        steps1, steps2, steps3 = sem("steps1"), sem("steps2"), sem("steps3")
        var1, var2, var3 = sem("var1"), sem("var2"), sem("var3")
        rstd1, rstd2, rstd3 = sem("rstd1"), sem("rstd2"), sem("rstd3")
        rstd2_kept = sem("rstd2_kept")
        bias1, affine3 = sem("bias1"), sem("affine3")
        signed = sem("signed")
        spread = [sem(f"spread{i}") for i in range(2)]
        conv1_done, relu_done, gated = sem("conv1_done"), sem("relu_done"), sem("gated")
        conv2_done, rounded, split = sem("conv2_done"), sem("rounded"), sem("split")
        acc0_ready, y_done, y_added, x1_ready = sem("acc0_ready"), sem("y_done"), sem("y_added"), sem("x1_ready")
        mask_bc = [sem(f"mask_bc{i}") for i in range(2)]
        u_ready, diag_ready, turned, maxed, pooled = (
            sem(n) for n in ("u_ready", "diag_ready", "turned", "maxed", "pooled"))
        mask_col = sem("mask_col")
        att_done, sigm, att_masked, mask_r_in, att_stored = (
            sem(n) for n in ("att_done", "sigm", "att_masked", "mask_r_in", "att_stored"))
        att_bc = [sem(f"att_bc{i}") for i in range(2)]
        o_ready, fin_relu, fin_added = sem("o_ready"), sem("fin_relu"), sem("fin_added")
        stored = [sem(f"stored{i}") for i in range(2)]

        def waits_apart(eng, a, *waits):
            if a.known:
                for s, count in waits:
                    wait(eng, s, count)
                return
            counts = [eng.to_reg(count) for _, count in waits]
            eng.wait_ge(cst_in, 16)
            for (s, _), count in zip(waits, counts):
                eng.wait_ge(s, count)

        block = ctx.enter_context(nc.Block())

        @block.sync
        def _(sp):
            def load_x(a):
                if not a.runs():
                    return
                waits_apart(sp, a, (x_in[a.par], a.half * 16))
                sp.dma_start(X[:, a.t, :], x_v[a.t]).then_inc(x_in[a.par], 16)

            def spread_signs(a):
                if not a.runs():
                    return
                waits_apart(sp, a, (signed, a.t + 1), (conv1_done, a.t * 4 - 4))
                for i in range(2):
                    src = U[64 * i:64 * i + 64, a.par, 0:PAD]
                    rows = list(src.ap[0])
                    same = bass.AP(src.tensor, src.offset, [rows, [0, 2], [1, PAD]])
                    moved = bass.AP(src.tensor, src.offset + 1, [rows, [PW - 1, 2], [1, PAD]])
                    sp.dma_start(R[0:64, a.par, i, :, :], same).then_inc(spread[a.par], 16)
                    sp.dma_start(R[64:128, a.par, i, :, :], moved).then_inc(spread[a.par], 16)

            def load_mask(a):
                if not a.runs():
                    return
                waits_apart(sp, a, (u_ready, a.t - 1))
                for i in range(2):
                    sp.dma_start(mask_b[64 * i:64 * i + 64, a.par, :],
                                 m_dram[a.t * 2 + i].partition_broadcast(64)).then_inc(mask_bc[a.par], 16)

            def load_mask_rows(a):
                if a.par == 0 or not a.runs():
                    return
                waits_apart(sp, a, (att_masked, a.half))
                sp.dma_start(mask_r[:, :], m_group[a.half])\
                  .then_inc(mask_r_in, 16)

            def store_attention(a):
                if a.par == 0 or not a.runs():
                    return
                waits_apart(sp, a, (att_masked, a.half + 1))
                sp.dma_start(a_group[a.half], att_m[:, :]).then_inc(att_stored, 16)

            def load_attention(a):
                if not a.runs():
                    return
                waits_apart(sp, a, (att_stored, (a.half + 1) * 16), (o_ready, a.t - 1))
                for i in range(2):
                    sp.dma_start(att_b[64 * i:64 * i + 64, a.par, :],
                                 a_dram[a.t * 2 + i].partition_broadcast(64)).then_inc(att_bc[a.par], 16)

            def store_out(a):
                if not a.runs():
                    return
                waits_apart(sp, a, (fin_added, a.t + 1))
                sp.dma_start(out_v[a.t], fin[:, a.par, :]).then_inc(stored[a.par], 16)

            def step(h, j):
                if not (isinstance(h, int) and h == 0):
                    load_x(Pair(h, j))
                if Pair(h, j - 8).par == 0:
                    load_attention(Pair(h, j - 8))
                    load_attention(Pair(h, j - 7))
                load_mask(Pair(h, j - 3))
                load_mask_rows(Pair(h, j - 6))
                store_out(Pair(h, j - 10))
                spread_signs(Pair(h, j - 1))
                store_attention(Pair(h, j - 6))

            sp.dma_start(w1f, w1).then_inc(w1_in, 16)
            load_x(Pair(0, 0))
            sp.dma_start(cs[:, :], cst).then_inc(cst_in, 16)
            load_x(Pair(0, 1))
            sp.dma_start(w2f, w2).then_inc(w2_in, 16)
            for k in range(3):
                step(k // 2, k % 2)
            for g in range(2):
                sp.wait_ge(mask_rows, g + 1)
                sp.dma_start(m_dram.rearrange("(g b) (j n) -> g (b j) n", g=2, n=CP)[g], mR[:, g, :])\
                  .then_inc(mask_stored, 16)
            sp.wait_ge(mask_stored, 32)
            for k in range(3, 12):
                step(k // 2, k % 2)
            with sp.Fori(12 // 2, NT // 2) as h:
                step(h, 0)
                step(h, 1)
            for k in range(NT, STEPS + 1):
                step(k // 2, k % 2)
            for i in range(2):
                sp.wait_ge(stored[i], NT // 2 * 16)

        @block.gpsimd
        def _(pool):
            pool.memset(mhalf[:, :], -0.5).then_inc(half_ready, 1)
            pool.memset(U[:, :, :], 0.0).then_inc(cleared, 1)
            pool.memset(S2[:, :, :, :, :], 0.0).then_inc(cleared, 1)
            pool.memset(red[:, :, :, :], 0.0).then_inc(cleared, 1)
            pool.wait_ge(half_ready, 1)
            pool.wait_ge(prep, 1)
            pool.tensor_tensor(rs[:, :], pv[:, :], mhalf[:, :], ALU.pow).then_inc(prep_pow, 1)
            pool.wait_ge(cst_in, 16)
            pool.wait_ge(cleared, 3)

            def power1(a):
                if a.runs():
                    pool.wait_ge(var1, a.t + 1)
                    wait(pool, acc0_ready, a.t - 1)
                    pool.tensor_tensor(r1[:, a.par:a.par + 1], ve1[:, a.par:a.par + 1], mhalf[:, 0:1],
                                       ALU.pow).then_inc(rstd1, 1)

            def power2(a):
                if not a.runs():
                    return
                pool.wait_ge(var2, a.t + 1)
                wait(pool, diag_ready, a.t - 1)
                wait(pool, rstd2_kept, a.t - 1)
                pool.tensor_tensor(r2p[:, a.par:a.par + 1], ve2[:, a.par:a.par + 1], mhalf[:, 0:1],
                                   ALU.pow).then_inc(rstd2, 1)
                waits_apart(pool, a, (rstd2, a.t + 1), (turned, a.t * 3 - 3))
                pool.tensor_scalar(diag[:, a.par, :], cs[:, K_ID:K_ID + P + 2], r2p[:, a.par:a.par + 1], 1.0,
                                   ALU.mult, ALU.mult).then_inc(diag_ready, 1)
                pool.tensor_copy(r2[:, bass.ds(a.t, 1)], r2p[:, a.par:a.par + 1]).then_inc(rstd2_kept, 1)

            def mask_column(a):
                if not a.runs():
                    return
                wait(pool, mask_mix, 8)
                wait(pool, att_done, a.half)
                pool.tensor_copy(red[:, 2, 1:NJ + 1, 2 * a.par:2 * a.par + 2].rearrange("p j b -> p b j"),
                                 mT[:, bass.ds(a.t * 2, 2), :])\
                    .then_inc(mask_col, 1)

            def mask_attention(a):
                if a.par == 0 or not a.runs():
                    return
                pool.wait_ge(sigm, a.half + 1)
                pool.wait_ge(mask_r_in, (a.half + 1) * 16)
                wait(pool, att_stored, a.half * 16)
                pool.tensor_tensor(att_m[:, :], att_s[:, :], mask_r[:, :], ALU.mult).then_inc(att_masked, 1)

            def power3(a):
                if a.runs():
                    pool.wait_ge(var3, a.t + 1)
                    wait(pool, affine3, a.t - 1)
                    pool.tensor_tensor(r3[:, a.par:a.par + 1], ve3[:, a.par:a.par + 1], mhalf[:, 0:1],
                                       ALU.pow).then_inc(rstd3, 1)

            def last_sum(a):
                if a.runs():
                    pool.wait_ge(fin_relu, a.t + 1)
                    pool.tensor_tensor(fin[:, a.par, :], fin[:, a.par, :], X[:, a.t, :], ALU.add)\
                        .then_inc(fin_added, 1)

            def step(h, j):
                mask_attention(Pair(h, j - 6))
                power1(Pair(h, j - 1))
                last_sum(Pair(h, j - 10))
                mask_column(Pair(h, j - 5))
                power3(Pair(h, j - 9))
                power2(Pair(h, j - 4))

            for k in range(12):
                step(k // 2, k % 2)
            with pool.Fori(12 // 2, NT // 2) as h:
                step(h, 0)
                step(h, 1)
            for k in range(NT, STEPS + 1):
                step(k // 2, k % 2)

        @block.scalar
        def _(act):
            act.dma_start(prm[:, :], par).then_inc(par_in, 16)
            act.dma_start(mfull[:, :, :], masks.rearrange("b h w -> h b w")).then_inc(mask_in, 16)
            act.dma_start(selz[:, :, :], sel).then_inc(att_in, 16)
            act.dma_start(atw[:, :], att_w).then_inc(att_in, 16)
            act.wait_ge(w1_in, 16)
            act.activation(w1s[:, :, :].rearrange("p k o -> p (k o)"), w1f, ACT.Sign).then_inc(w1_signs, 1)

            def sign_x(a):
                if not a.runs():
                    return
                wait(act, cleared, 1)
                act.wait_ge(mean1, a.t + 1)
                wait(act, spread[a.par], a.half * 64)
                act.activation(U[:, a.par, PW + 1:PW + 1 + H * PW].rearrange("p (h w) -> p h w", w=PW)[:, :, 0:W],
                               X[:, a.t, :].rearrange("p (h w) -> p h w", w=W), ACT.Sign,
                               bias=nm1[:, a.par:a.par + 1]).then_inc(signed, 1)

            def relu_unit(a, n):
                if not a.runs():
                    return
                act.wait_ge(conv1_done, a.t * 4 + n + 1)
                wait(act, gated, a.t * 4 + (n - 1) if n != 1 else a.t * 4)
                q = n % 2
                act.activation(relu[:, n % 2, :].rearrange("p (a n) -> p a n", a=2),
                               big[unit_slot((a.par + SKEW["c1"]) % 2, f"c1_{n}")][:, :, 0:HALF], ACT.Relu,
                               bias=shf[:, q:q + 1], scale=inv[:, q:q + 1]).then_inc(relu_done, 1)

            def start_sum(a):
                if not a.runs():
                    return
                act.wait_ge(bias1, a.t + 1)
                wait(act, y_added, a.t - 1)
                act.activation(acc0[:, a.par, :], X[:, a.t, :], ACT.Identity, bias=b1[:, a.par:a.par + 1],
                               scale=r1[:, a.par:a.par + 1]).then_inc(acc0_ready, 1)

            def sigmoid(a):
                if a.par == 0 or not a.runs():
                    return
                act.wait_ge(att_done, a.half + 1)
                wait(act, att_masked, a.half)
                act.activation(att_s[:, :], small[1][0:4 * NJ, 0:CP], ACT.Sigmoid).then_inc(sigm, 1)

            def last_relu(a):
                if not a.runs():
                    return
                act.wait_ge(affine3, a.t + 1)
                wait(act, stored[a.par], a.half * 16)
                act.activation(fin[:, a.par, :], o[:, a.par, :], ACT.Relu, bias=bi3[:, a.par:a.par + 1],
                               scale=sc3[:, a.par:a.par + 1]).then_inc(fin_relu, 1)

            def step(h, j):
                sigmoid(Pair(h, j - 6))
                relu_unit(Pair(h, j - 2), 0)
                sign_x(Pair(h, j - 1))
                relu_unit(Pair(h, j - 2), 1)
                start_sum(Pair(h, j - 3))
                relu_unit(Pair(h, j - 2), 2)
                relu_unit(Pair(h, j - 2), 3)
                last_relu(Pair(h, j - 9))

            for k in range(2):
                step(0, k)
            act.wait_ge(w2_in, 16)
            act.activation(w2s[:, :, :, :].rearrange("p q t o -> p (q t o)"), w2f, ACT.Sign).then_inc(w2_signs, 1)
            act.wait_ge(bn1_ready, 1)
            for k in range(2, 12):
                step(k // 2, k % 2)
            with act.Fori(12 // 2, NT // 2) as h:
                step(h, 0)
                step(h, 1)
            for k in range(NT, STEPS):
                step(k // 2, k % 2)

        @block.vector
        def _(dve):
            def stats_of(a, n, src, chain, done, mv):
                for i in range(2):
                    dve.bn_stats(bnst[:, n, i, :], src[:, HALF * i:HALF * (i + 1)]).then_inc(chain, 1)
                waits_apart(dve, a, (chain, a.t * 2 + 2))
                dve.bn_aggr(mv[:, a.par, :], bnst[:, n, :, :]).then_inc(done, 1)

            def stats_x(a):
                if not a.runs():
                    return
                waits_apart(dve, a, (x_in[a.par], (a.half + 1) * 16), (local1, a.t), (group1, a.t - 1),
                            (var1, a.t - 1))
                stats_of(a, 0, X[:, a.t, :], stats1, local1, mv1)

            def group_terms(a, mv, nm, ps, group, mean, chain, ve, var):
                dve.wait_ge(group, a.t + 1)
                dve.tensor_scalar(nm, ps[:, 0:1], -1.0, None, ALU.mult).then_inc(mean, 1)
                dve.tensor_scalar(tmp[:, 0:1], ps[:, 1:2], EPS, None, ALU.add).then_inc(chain, 1)
                dve.wait_ge(mean, a.t + 1)
                dve.tensor_tensor(dm[:, 0:1], mv[:, a.par, 0:1], nm, ALU.add).then_inc(chain, 1)
                dve.wait_ge(chain, a.t * 2 + 2)
                dve.scalar_tensor_tensor(ve[:, a.par:a.par + 1], dm[:, 0:1], dm[:, 0:1], tmp[:, 0:1],
                                         ALU.mult, ALU.add).then_inc(var, 1)

            def terms1(a):
                if not a.runs():
                    return
                wait(dve, signed, a.t - 1)
                wait(dve, rstd1, a.t - 1)
                wait(dve, bias1, a.t - 1)
                wait(dve, var1, a.t)
                group_terms(a, mv1, nm1[:, a.par:a.par + 1], small[1], group1, mean1, steps1, ve1, var1)

            def make_bias1(a):
                if not a.runs():
                    return
                dve.wait_ge(rstd1, a.t + 1)
                if a.known and a.t == 0:
                    dve.wait_ge(beta_ready, 1)
                wait(dve, acc0_ready, a.t - 1)
                dve.scalar_tensor_tensor(b1[:, a.par:a.par + 1], nm1[:, a.par:a.par + 1],
                                         r1[:, a.par:a.par + 1], beta[:, :], ALU.mult, ALU.add)\
                   .then_inc(bias1, 1)

            def gate(a, n):
                if not a.runs():
                    return
                dve.wait_ge(relu_done, a.t * 4 + n + 1)
                wait(dve, conv2_done, a.t * 2 - 2)
                i, q = n // 2, n % 2
                dst = S2[:, a.par, i, q, PW + 1:PW + 1 + (H - 1) * PW + W]
                dst = bass.AP(dst.tensor, dst.offset, [list(dst.ap[0]), [PW, H], [1, W]])
                dve.tensor_scalar(dst, relu[:, n % 2, :].rearrange("p (h w) -> p h w", w=W), 0.0, None,
                                  ALU.is_gt).then_inc(gated, 1)

            def split_sums(a, i):
                if not a.runs():
                    return
                dve.wait_ge(conv2_done, a.t * 2 + i + 1)
                wait(dve, y_done, a.t - 1)
                v = big[unit_slot((a.par + SKEW["c2"]) % 2, f"c2_{i}")][:, :, 0:HALF]
                whole = RD[:, a.par, i, 0, :].rearrange("p (a n) -> p a n", a=2)
                dve.tensor_scalar(whole, v, ROUND, ROUND, ALU.add, ALU.subtract).then_inc(rounded, 1)
                dve.wait_ge(rounded, a.t * 2 + i + 1)
                dve.tensor_tensor(RD[:, a.par, i, 1, :].rearrange("p (a n) -> p a n", a=2), whole, v,
                                  ALU.subtract).then_inc(split, 1)

            def finish_block(a):
                if not a.runs():
                    return
                dve.wait_ge(y_done, a.t + 1)
                dve.wait_ge(acc0_ready, a.t + 1)
                wait(dve, x1_ready, a.t)
                y = big[unit_slot((a.par + SKEW["y"]) % 2, "y")][:, :, 0:HALF]
                dve.tensor_tensor(ysum[:, :].rearrange("p (a n) -> p a n", a=2), y,
                                  acc0[:, a.par, :].rearrange("p (a n) -> p a n", a=2), ALU.add)\
                   .then_inc(y_added, 1)
                dve.wait_ge(y_added, a.t + 1)
                dve.scalar_tensor_tensor(X[:, a.t, :], ysum[:, :], 0.0, X[:, a.t, :], ALU.max, ALU.add)\
                   .then_inc(x1_ready, 1)
                waits_apart(dve, a, (x1_ready, a.t + 1), (local2, a.t), (group2, a.t - 1), (var2, a.t - 1))
                stats_of(a, 1, X[:, a.t, :], stats2, local2, mv2)

            def terms2(a):
                if not a.runs():
                    return
                wait(dve, var2, a.t)
                wait(dve, rstd2, a.t - 1)
                group_terms(a, mv2, nm2[:, bass.ds(a.t, 1)], small[0], group2, mean2, steps2, ve2, var2)

            def make_u(a):
                if not a.runs():
                    return
                dve.wait_ge(mask_bc[a.par], (a.half + 1) * 32)
                wait(dve, turned, a.t * 3 - 3)
                dve.scalar_tensor_tensor(u[:, a.par, :], X[:, a.t, :], nm2[:, bass.ds(a.t, 1)],
                                         mask_b[:, a.par, :], ALU.add, ALU.mult).then_inc(u_ready, 1)

            def reduce_chunks(a, n):
                if not a.runs():
                    return
                dve.wait_ge(turned, a.t * 3 + n + 1)
                wait(dve, att_done, a.half)
                j0, nj = 3 * n, min(3, NJ - 3 * n)
                ps = small[n % 2][0:CP, 0:nj * (P + 2)].rearrange("p (j m) -> p j m", m=P + 2)
                dst = [red[:, c, 1 + j0:1 + j0 + nj, 2 * a.par:2 * a.par + 2] for c in range(2)]
                dve.tensor_reduce(dst[1], ps[:, :, 0:P].rearrange("p j (i c) -> p j i c", i=2), AX_X, ALU.max)\
                   .then_inc(maxed, 1)
                dve.tensor_copy(dst[0], ps[:, :, P:P + 2]).then_inc(pooled, 1)

            def attend(a):
                if not a.runs():
                    return
                dve.wait_ge(att_bc[a.par], (a.half + 1) * 32)
                wait(dve, fin_relu, a.t - 1)
                dve.scalar_tensor_tensor(o[:, a.par, :], X[:, a.t, :], nm2[:, bass.ds(a.t, 1)],
                                         att_b[:, a.par, :], ALU.add, ALU.mult).then_inc(o_ready, 1)
                waits_apart(dve, a, (o_ready, a.t + 1))
                stats_of(a, 2, o[:, a.par, :], stats3, steps3, mv3)
                dve.wait_ge(steps3, a.t * 3 + 1)
                dve.wait_ge(rstd2_kept, a.t + 1)
                dve.tensor_scalar(tmp[:, 2:3], mv3[:, a.par, 1:2], r2[:, bass.ds(a.t, 1)], r2[:, bass.ds(a.t, 1)],
                                  ALU.mult, ALU.mult).then_inc(steps3, 1)
                dve.wait_ge(steps3, a.t * 3 + 2)
                dve.tensor_scalar(ve3[:, a.par:a.par + 1], tmp[:, 2:3], EPS, None, ALU.add).then_inc(var3, 1)

            def affine(a):
                if not a.runs():
                    return
                dve.wait_ge(rstd3, a.t + 1)
                dve.tensor_scalar(sc3[:, a.par:a.par + 1], r3[:, a.par:a.par + 1], r2[:, bass.ds(a.t, 1)],
                                  g5[:, 0:1], ALU.mult, ALU.mult).then_inc(steps3, 1)
                dve.wait_ge(steps3, a.t * 3 + 3)
                dve.scalar_tensor_tensor(bi3[:, a.par:a.par + 1], mv3[:, a.par, 0:1], sc3[:, a.par:a.par + 1],
                                         g5[:, 1:2], ALU.mult, ALU.subtract, reverse1=True)\
                   .then_inc(affine3, 1)

            def step(h, j):
                gate(Pair(h, j - 2), 0)
                split_sums(Pair(h, j - 4), 1)
                terms1(Pair(h, j - 1))
                make_bias1(Pair(h, j - 2))
                gate(Pair(h, j - 2), 1)
                finish_block(Pair(h, j - 4))
                reduce_chunks(Pair(h, j - 5), 0)
                gate(Pair(h, j - 2), 2)
                reduce_chunks(Pair(h, j - 5), 1)
                gate(Pair(h, j - 2), 3)
                reduce_chunks(Pair(h, j - 5), 2)
                stats_x(Pair(h, j))
                attend(Pair(h, j - 9))
                split_sums(Pair(h, j - 3), 0)
                terms2(Pair(h, j - 4))
                affine(Pair(h, j - 9))
                make_u(Pair(h, j - 4))

            n_prep = [0]

            def link(ins):
                n_prep[0] += 1
                ins.then_inc(prep, 1)
                dve.wait_ge(prep, n_prep[0])

            def scales():
                dve.wait_ge(par_in, 16)
                link(dve.tensor_scalar(pv[:, :], prm[:, Q_VAR:Q_VAR + 4], EPS, None, ALU.add))
                dve.wait_ge(prep_pow, 1)
                link(dve.tensor_tensor(inv[:, :], prm[:, Q_SCALE:Q_SCALE + 4], rs[:, :], ALU.mult))
                link(dve.tensor_tensor(tmp[:, :], prm[:, Q_MEAN:Q_MEAN + 4], inv[:, :], ALU.mult))
                dve.tensor_tensor(shf[:, :], prm[:, Q_BIAS:Q_BIAS + 4], tmp[:, :], ALU.subtract)\
                   .then_inc(bn1_ready, 1)
                dve.wait_ge(bn1_ready, 1)
                link(dve.tensor_tensor(kap[:, :], shf[:, 2:4], prm[:, Q_LAM:Q_LAM + 2], ALU.mult))
                dve.tensor_tensor(kaps[:, :], kap[:, 0:1], kap[:, 1:2], ALU.add).then_inc(beta_sum, 1)
                link(dve.tensor_tensor(alpha[:, 0:1], inv[:, 3:4], prm[:, Q_LAM + 1:Q_LAM + 2], ALU.mult))
                link(dve.tensor_scalar(alpha[:, 1:2], inv[:, 2:3], prm[:, Q_LAM:Q_LAM + 1], -SHIFT,
                                       ALU.mult, ALU.mult))
                link(dve.tensor_copy(part[:, 0, :], alpha[:, :]))
                link(dve.tensor_tensor(rest[:, 0, :], alpha[:, :], part[:, 0, :], ALU.subtract))
                link(dve.tensor_copy(part[:, 1, :], rest[:, 0, :]))
                link(dve.tensor_tensor(rest[:, 1, :], rest[:, 0, :], part[:, 1, :], ALU.subtract))
                link(dve.tensor_copy(part[:, 2, :], rest[:, 1, :]))
                link(dve.tensor_scalar(g5[:, :], prm[:, Q_GAMMA:Q_GAMMA + 2], SELECTED, None, ALU.mult))

            def mix_weights():
                dve.wait_ge(cst_in, 16)
                for kind in range(2):
                    for n in range(3):
                        dve.tensor_scalar(wa[:, kind, n, :], cs[:, K_SEL:K_SEL + 64],
                                          part[:, n, kind:kind + 1], None, ALU.mult).then_inc(mix_ready, 1)
                dve.wait_ge(beta_sum, 2)
                dve.tensor_copy(beta[:, :], small[0][:, 0:1]).then_inc(beta_ready, 1)

            def scale_w2():
                dve.wait_ge(w2_signs, 1)
                dve.tensor_scalar(w2t[:, :, :, :].rearrange("p q t o -> p (q t o)"),
                                  w2s[:, :, :, :].rearrange("p q t o -> p (q t o)"),
                                  cs[:, K_SCALE:K_SCALE + 1], None, ALU.mult).then_inc(w2_ready, 1)

            def mask_work():
                dve.wait_ge(mask_h, 1)
                dve.tensor_copy(mh[:, :, :].rearrange("p b h -> p (b h)"), big[2][:, 0, 0:MB * H])\
                   .then_inc(mask_hs, 1)
                dve.wait_ge(mask_hw, 1)
                ps = big[2][0:CP, 1, 0:MB * NJ].rearrange("p (b j) -> p b j", j=NJ)
                dve.tensor_copy(mhw[:, 1:MB + 1, :], ps).then_inc(mask_hs, 1)
                dve.tensor_copy(mhw[:, 0, :], ps[:, 0, :]).then_inc(mask_hs, 1)
                dve.tensor_copy(mhw[:, MB + 1, :], ps[:, MB - 1, :]).then_inc(mask_hs, 1)
                dve.wait_ge(mask_hs, 4)
                n_r = B // MB
                m_v = mT[:, :, :].rearrange("p (b r) j -> p b r j", r=n_r)
                for r in range(n_r):
                    at = (r + 0.5) / n_r - 0.5
                    lo = 0 if at < 0 else 1
                    hi_w = at + 1 if at < 0 else at
                    dve.tensor_scalar(mlo[:, :, :], mhw[:, lo:lo + MB, :], 1.0 - hi_w, None, ALU.mult)\
                       .then_inc(mask_mix, 1)
                    dve.wait_ge(mask_mix, 2 * r + 1)
                    dve.scalar_tensor_tensor(m_v[:, :, r, :], mhw[:, lo + 1:lo + 1 + MB, :], hi_w, mlo[:, :, :],
                                             ALU.mult, ALU.add).then_inc(mask_mix, 1)
                    dve.wait_ge(mask_mix, 2 * r + 2)
                for g in range(2):
                    dve.wait_ge(mask_turned, g + 1)
                    dve.tensor_copy(mR[:, g, :], big[2][0:CP, g, 0:CP]).then_inc(mask_rows, 1)

            def band_work():
                dve.wait_ge(band_made, 1)
                n = NCH * 3 * CH
                for i in range(2):
                    dve.tensor_copy(band[:, :, RH * i:RH * (i + 1)],
                                    big[1][0:CP, i, 0:RH * n].rearrange("p (w c) -> p c w", c=n))\
                       .then_inc(band_ready, 1)

            step(0, 0)
            scales()
            step(0, 1)
            dve.wait_ge(cleared, 3)
            mix_weights()
            scale_w2()
            mask_work()
            band_work()
            for k in range(2, 12):
                step(k // 2, k % 2)
            with dve.Fori(12 // 2, NT // 2) as h:
                step(h, 0)
                step(h, 1)
            for k in range(NT, STEPS):
                step(k // 2, k % 2)

        @block.tensor
        def _(pe):
            def group_stats(a, mv, local, ps, group):
                pe.wait_ge(local, a.t + 1)
                pe.matmul(ps[:, 0:2], cs[:, K_PAIR:K_PAIR + P], mv[:, a.par, :], start=True, stop=True)\
                  .then_inc(group, 1)

            def after_sigmoid(h, off):
                b = Pair(h, off if off % 2 else off - 1)
                if b.runs():
                    pe.wait_ge(sigm, b.half + 1)

            def stats_x(a):
                if not a.runs():
                    return
                b = Pair(a.h, a.off - 5)
                if b.runs():
                    pe.wait_ge(pooled, b.t * 3 + 2)
                after_sigmoid(a.h, a.off - 5)
                wait(pe, var1, a.t)
                group_stats(a, mv1, local1, small[1], group1)

            def stats_x1(a):
                if not a.runs():
                    return
                b = Pair(a.h, a.off - 1)
                if b.runs():
                    pe.wait_ge(pooled, b.t * 3 + 3)
                group_stats(a, mv2, local2, small[0], group2)

            def free_big(name, h, j):
                known = isinstance(h, int)
                found = unit_before(known, 2 * h + j if known else None, j, name)
                if not found:
                    return
                back, other = found
                kind = other.split("_")[0]
                b = Pair(h, j - back - SKEW[kind])
                if kind == "c1":
                    pe.wait_ge(relu_done, b.t * 4 + int(other[-1]) + 1)
                elif kind == "c2":
                    pe.wait_ge(split, b.t * 2 + int(other[-1]) + 1)
                else:
                    pe.wait_ge(y_added, b.t + 1)

            def window(row0, dy, dx, src):
                at = (row0 + dy) * PW + dx
                return bass.AP(src.tensor, src.offset + at, [list(src.ap[0]), [PW, RH], [1, W]])

            def conv1(h, j, n):
                a = Pair(h, j - SKEW["c1"])
                if not a.runs():
                    return
                free_big(f"c1_{n}", h, j)
                pe.wait_ge(spread[a.par], (a.half + 1) * 64)
                i, q = n // 2, n % 2
                acc = big[unit_slot(j, f"c1_{n}")]
                taps = [(1, 0, 0), (1, 0, 1), (1, 0, 2), (0, 2, 0), (0, 2, 2)]
                for hh in range(2):
                    for s, (copy, dy, dx) in enumerate(taps):
                        mm = pe.matmul(acc[:, hh, 0:HALF], w1s[:, s, q * P:(q + 1) * P],
                                       window(RH * hh, dy, dx, R[:, a.par, i, copy, :]),
                                       start=(s == 0), stop=(s == KS - 1))
                mm.then_inc(conv1_done, 1)

            def conv2(h, j, i):
                a = Pair(h, j - SKEW["c2"])
                if not a.runs():
                    return
                free_big(f"c2_{i}", h, j)
                pe.wait_ge(gated, a.t * 4 + 2 * i + 2)
                acc = big[unit_slot(j, f"c2_{i}")]
                for hh in range(2):
                    for t in range(9):
                        for q in range(2):
                            mm = pe.matmul(acc[64 * q:64 * q + 64, hh, 0:HALF], w2t[:, q, t, :],
                                           window(RH * hh, t // 3, t % 3, S2[:, a.par, i, q, :]),
                                           start=(t == 0), stop=(t == 8))
                mm.then_inc(conv2_done, 1)

            def mix(h, j):
                a = Pair(h, j - SKEW["y"])
                if not a.runs():
                    return
                free_big("y", h, j)
                pe.wait_ge(split, a.t * 2 + 2)
                acc = big[unit_slot(j, "y")]
                for hh in range(2):
                    for m in range(6):
                        for i in range(2):
                            mm = pe.matmul(acc[64 * i:64 * i + 64, hh, 0:HALF], wa[:, m // 3, m % 3, :],
                                           RD[:, a.par, i, m // 3, HALF * hh:HALF * (hh + 1)],
                                           start=(m == 0), stop=(m == 5))
                mm.then_inc(y_done, 1)

            def turn(a, n):
                if not a.runs():
                    return
                if n == 0:
                    pe.wait_ge(u_ready, a.t + 1)
                    pe.wait_ge(diag_ready, a.t + 1)
                elif n == 1:
                    after_sigmoid(a.h, a.off - 1)
                    b = Pair(a.h, a.off + 4)
                    if b.runs():
                        pe.wait_ge(var1, b.t + 1)
                else:
                    pe.wait_ge(pooled, a.t * 3 + 1)
                for j in range(3 * n, min(3 * n + 3, NJ)):
                    at = (j - 3 * n) * (P + 2)
                    mm = pe.matmul(small[n % 2][0:CP, at:at + P + 2], u[:, a.par, CP * j:CP * (j + 1)],
                                   diag[:, a.par, :], start=True, stop=True)
                mm.then_inc(turned, 1)

            def attention(a):
                if a.par == 0 or not a.runs():
                    return
                pe.wait_ge(pooled, a.t * 3 + 3)
                pe.wait_ge(mask_col, a.t + 1)
                b = Pair(a.h, a.off + 4)
                if b.runs():
                    pe.wait_ge(var1, b.t + 1)
                for m in range(9):
                    c, dj = m // 3, m % 3
                    mm = pe.matmul(small[1][0:4 * NJ, 0:CP], red[:, c, dj:dj + NJ, :].rearrange("p j b -> p (j b)"),
                                   band[:, m * CH:(m + 1) * CH, :].rearrange("p k w -> p (k w)"),
                                   start=(m == 0), stop=(m == 8))
                mm.then_inc(att_done, 1)

            def step(h, j):
                def at(skew):
                    a = Pair(h, j - skew)
                    a.h, a.off = h, j - skew
                    return a
                attention(at(6))
                conv1(h, j, 0)
                stats_x(at(1))
                conv1(h, j, 1)
                mix(h, j)
                turn(at(5), 0)
                conv1(h, j, 2)
                turn(at(5), 1)
                conv1(h, j, 3)
                turn(at(5), 2)
                conv2(h, j, 0)
                stats_x1(at(4))
                conv2(h, j, 1)

            def resize_mask():
                pe.wait_ge(mask_in, 16)
                for b in range(MB):
                    mm = pe.matmul(big[2][:, 0, b * H:(b + 1) * H], mfull[:, b, :], cs[:, K_RH:K_RH + H],
                                   start=True, stop=True)
                mm.then_inc(mask_h, 1)

            def resize_mask_w():
                pe.wait_ge(mask_hs, 1)
                for k in range(CH):
                    mm = pe.matmul(big[2][0:CP, 1, 0:MB * NJ], cs[:, K_RW + CP * k:K_RW + CP * (k + 1)],
                                   mh[:, :, k:H:CH], start=(k == 0), stop=(k == CH - 1))
                mm.then_inc(mask_hw, 1)

            def band_matrices():
                pe.wait_ge(att_in, 32)
                n = NCH * 3 * CH
                for w in range(W):
                    mm = pe.matmul(big[1][0:CP, w // RH, (w % RH) * n:(w % RH + 1) * n],
                                   selz[:, w, :], atw[:, :], start=True, stop=True)
                mm.then_inc(band_made, 1)

            def turn_mask():
                pe.wait_ge(mask_mix, 8)
                for g in range(2):
                    pe.matmul(big[2][0:CP, g, 0:CP], mT[:, 16 * g:16 * g + 16, :].rearrange("p b j -> p (b j)"),
                              cs[0:CP, K_ID:K_ID + CP], start=True, stop=True).then_inc(mask_turned, 1)

            pe.wait_ge(cst_in, 16)
            step(0, 0)
            step(0, 1)
            resize_mask()
            pe.wait_ge(beta_sum, 1)
            pe.matmul(small[0][:, 0:1], cs[:, K_FOLD:K_FOLD + P], kaps[:, :], start=True, stop=True)\
              .then_inc(beta_sum, 1)
            resize_mask_w()
            band_matrices()
            turn_mask()
            pe.wait_ge(mask_rows, 2)
            pe.wait_ge(band_ready, 2)
            pe.wait_ge(beta_ready, 1)
            pe.wait_ge(w1_signs, 1)
            step(1, 0)
            pe.wait_ge(w2_ready, 1)
            pe.wait_ge(mix_ready, 6)
            for k in range(3, 10):
                step(k // 2, k % 2)
            with pe.Fori(10 // 2, NT // 2) as h:
                step(h, 0)
                step(h, 1)
            for k in range(NT, STEPS):
                step(k // 2, k % 2)


def resize_weights(n_in, n_out):
    f = np.float32
    inv = f(1.0) / f(n_out / n_in)
    kernel = max(inv, f(1.0))
    at = (np.arange(n_out, dtype=f) + f(0.5)) * inv - f(0.5)
    w = np.maximum(f(0), f(1) - np.abs(at[None, :] - np.arange(n_in, dtype=f)[:, None]) / kernel)
    return (w / w.sum(axis=0, keepdims=True)).astype(f)


def constants():
    cst = np.zeros((P, K_N), np.float32)
    cst[:, K_ID:K_ID + P] = np.eye(P)
    ch = np.arange(P)
    for i in range(2):
        cst[64 * i:64 * i + 64, K_MEAN + i] = 1.0 / C
    cst[:, K_PAIR:K_PAIR + P] = 0.5 * (ch[:, None] // 2 == ch[None, :] // 2)
    cst[:, K_FOLD:K_FOLD + P] = ch[:, None] % 64 == ch[None, :] % 64
    cst[:, K_SEL:K_SEL + 64] = ch[:, None] % 64 == ch[None, :64]
    cst[:, K_RH:K_RH + H] = resize_weights(MH, H)
    for k in range(CH):
        cst[:, K_RW + CP * k + W * k:K_RW + CP * k + W * (k + 1)] = resize_weights(MW, W)
    cst[:, K_SCALE] = np.where(ch < 64, 1.0 / SHIFT, 1.0)
    sel = np.zeros((CH, KW, W, CH, W), np.float32)
    for k in range(CH):
        for dx in range(KW):
            sel[k, dx, :, k, :] = np.eye(W, k=dx - 3)
    return cst, sel.reshape(CH * KW, W, CP)


def kernel(x, L0_conv_w1, L0_conv_bn1_scale, L0_conv_bn1_bias, L0_conv_bn1_mean, L0_conv_bn1_var, L0_conv_w2,
           L0_conv_bn2_scale, L0_conv_bn2_bias, L0_conv_bn2_mean, L0_conv_bn2_var, L0_conv_lambdas,
           L1_conv_masks, L1_conv_conv_w, L1_conv_in_gamma, L1_conv_in_beta):
    import concourse.bacc as bacc
    from concourse.bass_utils import run_bass_kernel_spmd

    w1 = np.asarray(L0_conv_w1).transpose(1, 2, 3, 0)
    w1_l = np.zeros((2, C, KS, G * 64), np.float32)
    for dx in range(3):
        w1_l[0, :, dx] = w1[:, 0, dx]
        w1_l[1, :, dx] = w1[:, 1, dx]
    w1_l[0, :, 3], w1_l[1, :, 3], w1_l[0, :, 4] = w1[:, 2, 0], w1[:, 2, 1], w1[:, 2, 2]
    w2 = np.asarray(L0_conv_w2).reshape(2, 2, 64, C, 9)
    w2_l = np.ascontiguousarray(w2.transpose(1, 3, 0, 4, 2)).reshape(P, 2 * 9 * 64)
    prm = np.zeros((P, Q_N), np.float32)
    for at, one, two in ((Q_SCALE, L0_conv_bn1_scale, L0_conv_bn2_scale), (Q_BIAS, L0_conv_bn1_bias, L0_conv_bn2_bias),
                         (Q_MEAN, L0_conv_bn1_mean, L0_conv_bn2_mean), (Q_VAR, L0_conv_bn1_var, L0_conv_bn2_var)):
        prm[:, at:at + 2] = np.asarray(one).reshape(2, P).T
        prm[:, at + 2:at + 4] = np.asarray(two).reshape(2, 2, 64).transpose(0, 2, 1).reshape(P, 2)
    prm[:, Q_LAM:Q_LAM + 2] = np.repeat(np.asarray(L0_conv_lambdas).reshape(2, 2), 64, axis=0)
    prm[:, Q_GAMMA] = np.tile(np.asarray(L1_conv_in_gamma), 2)
    prm[:, Q_BETA] = np.tile(np.asarray(L1_conv_in_beta), 2)
    cw = np.asarray(L1_conv_conv_w)[0]
    att = np.zeros((CH, KW, NCH, 3, CH), np.float32)
    for kin in range(CH):
        for dj in range(3):
            for k in range(CH):
                dy = CH * (dj - 1) + kin - k + 3
                if 0 <= dy < KW:
                    att[kin, :, :, dj, k] = cw[:, dy, :].T
    cst, sel = constants()
    arrays = {
        "x": np.asarray(x), "w1": w1_l.reshape(P, KS * G * 64), "w2": w2_l, "par": prm,
        "masks": np.asarray(L1_conv_masks), "att_w": att.reshape(CH * KW, NCH * 3 * CH), "cst": cst, "sel": sel,
    }
    nc = bacc.Bacc("TRN2", target_bir_lowering=False, num_devices=1)
    args = {n: nc.dram_tensor(f"in_{n}", a.shape, mybir.dt.from_np(a.dtype), kind="ExternalInput").ap()
            for n, a in arrays.items()}
    out = nc.dram_tensor("out", (B, C, H, W), F32, kind="ExternalOutput").ap()
    build(nc, *args.values(), out)
    r = run_bass_kernel_spmd(nc, [{f"in_{n}": a for n, a in arrays.items()}], core_ids=[0])
    return r.results[0]["out"]
```

```python
from contextlib import ExitStack

import numpy as np

import concourse.bass as bass
from concourse import mybir

ALU = mybir.AluOpType
ACT = mybir.ActivationFunctionType
AX_X = mybir.AxisListType.X
F32 = mybir.dt.float32
BF16 = mybir.dt.bfloat16
F16 = mybir.dt.float16

P = 128
B, C, H, W = 32, 64, 28, 28
HW = H * W
HALF = HW // 2
RH = H // 2
NT = B // 2
G = 4
PW = W + 2
PAD = (H + 2) * PW
PADX = PAD + 32
KS = 5
CH = 4
CP = CH * W
NJ = H // CH
MB, MH, MW = 8, 128, 128
KW = 7
NCH = 3
EPS = 1e-5
ROUND = 1.5 * 2.0 ** 23
SHIFT = 2.0 ** 11
SELECTED = 5.0

K_ID = 0
K_MEAN = K_ID + P
K_PAIR = K_MEAN + 2
K_FOLD = K_PAIR + P
K_SEL = K_FOLD + P
K_RH = K_SEL + 64
K_RW = K_RH + H
K_SCALE = K_RW + CH * CP
K_N = K_SCALE + 1
Q_SCALE, Q_BIAS, Q_MEAN, Q_VAR, Q_LAM, Q_GAMMA, Q_BETA, Q_N = 0, 4, 8, 12, 16, 18, 19, 20

LAST_SKEW = 7
STEPS = NT + LAST_SKEW
FIRST_LOOP = 10


class Pair:

    def __init__(self, h, off):
        self.known = isinstance(h, int)
        self.t = h * 2 + off if off else h * 2
        self.half = h + off // 2 if off // 2 else h
        self.par = off % 2

    def runs(self):
        return not self.known or 0 <= self.t < NT


def wait(eng, sem, count):
    if isinstance(count, int) and count <= 0:
        return
    eng.wait_ge(sem, count)


UNITS = ["c1_0", "c1_1", "c2_0", "y", "c1_2", "c1_3", "c2_1"]
SKEW = {"c1": 1, "y": 3, "c2": 2}


def unit_slot(par, name):
    return (len(UNITS) * par + UNITS.index(name)) % 3


def unit_before(step_known, k, par, name):
    back, pos = 0, UNITS.index(name)
    slot = unit_slot(par, name)
    while True:
        pos -= 1
        if pos < 0:
            pos, back = len(UNITS) - 1, back + 1
        if step_known and k - back < 0:
            return None
        other = UNITS[pos]
        if unit_slot((par - back) % 2, other) != slot:
            continue
        if step_known and not 0 <= k - back - SKEW[other.split("_")[0]] < NT:
            continue
        return back, other


def build(nc, x, w1, w2, par, masks, att_w, cst, sel, out):
    x_v = x.rearrange("(t i) c h w -> t (i c) (h w)", i=2)
    out_v = out.rearrange("(t i) c h w -> t (i c) (h w)", i=2)
    m_dram = nc.dram_tensor("mask_rows", (B, HW), F32, kind="Internal").ap()
    a_dram = nc.dram_tensor("attention_rows", (B, HW), F32, kind="Internal").ap()
    m_group = m_dram.rearrange("(g b) (j n) -> g j b n", b=4, n=CP)
    a_group = a_dram.rearrange("(g b) (j n) -> g j b n", b=4, n=CP)

    ctx = ExitStack()
    with ctx:
        def sb(name, shape, dt):
            return ctx.enter_context(nc.sbuf_tensor(name, shape, dt))

        def sem(name):
            return ctx.enter_context(nc.semaphore(name))

        X = sb("X", [P, NT, HW], F32)
        U = sb("U", [P, 2, PADX], BF16)
        R = sb("R", [P, 2, 2, 2, PAD], BF16)
        relu = sb("relu", [P, G, HW], BF16)
        S2 = sb("S2", [P, 2, 2, 2, PAD], BF16)
        RD = sb("RD", [P, 2, 2, 2, HW], F16)
        acc0 = sb("acc0", [P, 2, HW], F32)
        ysum = sb("ysum", [P, HW], F32)
        mask_b = sb("mask_b", [P, 2, HW], F32)
        u = sb("u", [P, 2, HW], F32)
        diag = sb("diag", [P, 2, P + 2], F32)
        att_b = sb("att_b", [P, 2, HW], F32)
        o = sb("o", [P, 2, HW], F32)
        fin = sb("fin", [P, 2, HW], F32)
        red = sb("red", [CP, NCH, NJ + 2, 4], F32)
        att_s = sb("att_s", [4 * NJ, CP], F32)
        att_m = sb("att_m", [4 * NJ, CP], F32)
        mask_r = sb("mask_r", [4 * NJ, CP], F32)
        bnst = sb("bnst", [P, 3, 2, 6], F32)
        mv1 = sb("mv1", [P, 2, 2], F32)
        mv2 = sb("mv2", [P, 2, 2], F32)
        mv3 = sb("mv3", [P, 2, 2], F32)
        nm1 = sb("nm1", [P, 2], F32)
        ve1 = sb("ve1", [P, 2], F32)
        r1 = sb("r1", [P, 2], F32)
        b1 = sb("b1", [P, 2], F32)
        dm = sb("dm", [P, 2], F32)
        nm2 = sb("nm2", [P, NT], F32)
        ve2 = sb("ve2", [P, 2], F32)
        r2p = sb("r2p", [P, 2], F32)
        r2 = sb("r2", [P, NT], F32)
        ve3 = sb("ve3", [P, 2], F32)
        r3 = sb("r3", [P, 2], F32)
        sc3 = sb("sc3", [P, 2], F32)
        bi3 = sb("bi3", [P, 2], F32)
        tmp = sb("tmp", [P, 4], F32)
        w1s = sb("w1s", [P, KS, 2 * P], BF16)
        w2s = sb("w2s", [P, 2, 9, 64], BF16)
        w2t = sb("w2t", [P, 2, 9, 64], BF16)
        wa = sb("wa", [P, 2, 3, 64], BF16)
        cs = sb("cs", [P, K_N], F32)
        selz = sb("selz", [CH * KW, W, CP], F32)
        atw = sb("atw", [CH * KW, NCH * 3 * CH], F32)
        band = sb("band", [CP, NCH * 3 * CH, W], F32)
        prm = sb("prm", [P, Q_N], F32)
        pv = sb("pv", [P, 4], F32)
        rs = sb("rs", [P, 4], F32)
        inv = sb("inv", [P, 4], F32)
        shf = sb("shf", [P, 4], F32)
        alpha = sb("alpha", [P, 2], F32)
        rest = sb("rest", [P, 2, 2], F32)
        part = sb("part", [P, 3, 2], BF16)
        kap = sb("kap", [P, 2], F32)
        kaps = sb("kaps", [P, 1], F32)
        beta = sb("beta", [P, 1], F32)
        g5 = sb("g5", [P, 2], F32)
        mhalf = sb("mhalf", [P, 4], F32)
        mfull = sb("mfull", [MH, MB, MW], F32)
        mh = sb("mh", [MW, MB, H], F32)
        mhw = sb("mhw", [CP, MB + 2, NJ], F32)
        mlo = sb("mlo", [CP, MB, NJ], F32)
        mT = sb("mT", [CP, B, NJ], F32)
        mR = sb("mR", [CP, 2, CP], F32)
        w1f = o[:, :, :].rearrange("p a n -> p (a n)")[:, 0:KS * 2 * P]
        w2f = fin[:, :, :].rearrange("p a n -> p (a n)")[:, 0:2 * 9 * 64]

        big = [ctx.enter_context(nc.psum_tensor(f"big{i}", [P, 2, 512], F32)) for i in range(3)]
        small = [ctx.enter_context(nc.psum_tensor(f"small{i}", [P, 512], F32)) for i in range(2)]

        x_in = [sem(f"x_in{i}") for i in range(2)]
        w1_in, w2_in, par_in, cst_in, mask_in, att_in = (
            sem(n) for n in ("w1_in", "w2_in", "par_in", "cst_in", "mask_in", "att_in"))
        w1_signs, w2_signs, w2_ready = sem("w1_signs"), sem("w2_signs"), sem("w2_ready")
        cleared, prep, prep_pow, bn1_ready = sem("cleared"), sem("prep"), sem("prep_pow"), sem("bn1_ready")
        mix_ready, beta_ready, beta_sum = sem("mix_ready"), sem("beta_ready"), sem("beta_sum")
        mask_h, mask_hs, mask_hw, mask_mix, mask_turned, mask_rows = (
            sem(n) for n in ("mask_h", "mask_hs", "mask_hw", "mask_mix", "mask_turned", "mask_rows"))
        mask_stored, band_made, band_ready, half_ready = (
            sem(n) for n in ("mask_stored", "band_made", "band_ready", "half_ready"))
        stats1, stats2, stats3 = sem("stats1"), sem("stats2"), sem("stats3")
        local1, local2 = sem("local1"), sem("local2")
        group1, group2 = sem("group1"), sem("group2")
        mean1, mean2 = sem("mean1"), sem("mean2")
        steps1, steps2, steps3 = sem("steps1"), sem("steps2"), sem("steps3")
        var1, var2, var3 = sem("var1"), sem("var2"), sem("var3")
        rstd1, rstd2, rstd3 = sem("rstd1"), sem("rstd2"), sem("rstd3")
        rstd2_kept = sem("rstd2_kept")
        bias1, affine3 = sem("bias1"), sem("affine3")
        signed = sem("signed")
        spread = [sem(f"spread{i}") for i in range(2)]
        conv1_done, relu_done, gated = sem("conv1_done"), sem("relu_done"), sem("gated")
        conv2_done, rounded, split = sem("conv2_done"), sem("rounded"), sem("split")
        acc0_ready, y_done, y_added, x1_ready = sem("acc0_ready"), sem("y_done"), sem("y_added"), sem("x1_ready")
        mask_bc = [sem(f"mask_bc{i}") for i in range(2)]
        u_ready, diag_ready, turned, maxed, pooled = (
            sem(n) for n in ("u_ready", "diag_ready", "turned", "maxed", "pooled"))
        mask_col = sem("mask_col")
        att_done, sigm, att_masked, mask_r_in, att_stored = (
            sem(n) for n in ("att_done", "sigm", "att_masked", "mask_r_in", "att_stored"))
        att_bc = [sem(f"att_bc{i}") for i in range(2)]
        o_ready, fin_relu, fin_added = sem("o_ready"), sem("fin_relu"), sem("fin_added")
        stored = [sem(f"stored{i}") for i in range(2)]

        def waits_apart(eng, a, *waits):
            if a.known:
                for s, count in waits:
                    wait(eng, s, count)
                return
            counts = [eng.to_reg(count) for _, count in waits]
            eng.wait_ge(cst_in, 16)
            for (s, _), count in zip(waits, counts):
                eng.wait_ge(s, count)

        block = ctx.enter_context(nc.Block())

        @block.sync
        def _(sp):
            def load_x(a):
                if not a.runs():
                    return
                waits_apart(sp, a, (x_in[a.par], a.half * 16))
                sp.dma_start(X[:, a.t, :], x_v[a.t]).then_inc(x_in[a.par], 16)

            def spread_signs(a):
                if not a.runs():
                    return
                waits_apart(sp, a, (signed, a.t + 1), (conv1_done, a.t * 4 - 4))
                for i in range(2):
                    src = U[64 * i:64 * i + 64, a.par, 0:PAD]
                    rows = list(src.ap[0])
                    same = bass.AP(src.tensor, src.offset, [rows, [0, 2], [1, PAD]])
                    moved = bass.AP(src.tensor, src.offset + 1, [rows, [PW - 1, 2], [1, PAD]])
                    sp.dma_start(R[0:64, a.par, i, :, :], same).then_inc(spread[a.par], 16)
                    sp.dma_start(R[64:128, a.par, i, :, :], moved).then_inc(spread[a.par], 16)

            def load_mask(a):
                if not a.runs():
                    return
                waits_apart(sp, a, (u_ready, a.t - 1))
                for i in range(2):
                    sp.dma_start(mask_b[64 * i:64 * i + 64, a.par, :],
                                 m_dram[a.t * 2 + i].partition_broadcast(64)).then_inc(mask_bc[a.par], 16)

            def load_mask_rows(a):
                if a.par == 0 or not a.runs():
                    return
                waits_apart(sp, a, (att_masked, a.half))
                sp.dma_start(mask_r[:, :], m_group[a.half])\
                  .then_inc(mask_r_in, 16)

            def store_attention(a):
                if a.par == 0 or not a.runs():
                    return
                waits_apart(sp, a, (att_masked, a.half + 1))
                sp.dma_start(a_group[a.half], att_m[:, :]).then_inc(att_stored, 16)

            def load_attention(a):
                if not a.runs():
                    return
                waits_apart(sp, a, (att_stored, (a.half + 1) * 16), (o_ready, a.t - 1))
                for i in range(2):
                    sp.dma_start(att_b[64 * i:64 * i + 64, a.par, :],
                                 a_dram[a.t * 2 + i].partition_broadcast(64)).then_inc(att_bc[a.par], 16)

            def store_out(a):
                if not a.runs():
                    return
                waits_apart(sp, a, (fin_added, a.t + 1))
                sp.dma_start(out_v[a.t], fin[:, a.par, :]).then_inc(stored[a.par], 16)

            def step(h, j):
                load_x(Pair(h, j + 2))
                load_mask_rows(Pair(h, j - 4))
                load_mask(Pair(h, j - 3))
                store_attention(Pair(h, j - 5))
                if Pair(h, j - 5).par == 1:
                    load_attention(Pair(h, j - 6))
                    load_attention(Pair(h, j - 5))
                spread_signs(Pair(h, j))
                store_out(Pair(h, j - 7))

            sp.dma_start(w1f, w1).then_inc(w1_in, 16)
            load_x(Pair(0, 0))
            sp.dma_start(cs[:, :], cst).then_inc(cst_in, 16)
            load_x(Pair(0, 1))
            sp.dma_start(w2f, w2).then_inc(w2_in, 16)
            for k in range(2):
                step(0, k)
            for g in range(2):
                sp.wait_ge(mask_rows, g + 1)
                sp.dma_start(m_dram.rearrange("(g b) (j n) -> g (b j) n", g=2, n=CP)[g], mR[:, g, :])\
                  .then_inc(mask_stored, 16)
            sp.wait_ge(mask_stored, 32)
            for k in range(2, FIRST_LOOP):
                step(k // 2, k % 2)
            with sp.Fori(FIRST_LOOP // 2, (NT - 2) // 2) as h:
                step(h, 0)
                step(h, 1)
            for k in range(NT - 2, STEPS):
                step(k // 2, k % 2)
            for i in range(2):
                sp.wait_ge(stored[i], NT // 2 * 16)

        @block.gpsimd
        def _(pool):
            pool.memset(mhalf[:, :], -0.5).then_inc(half_ready, 1)
            pool.memset(U[:, :, :], 0.0).then_inc(cleared, 1)
            pool.memset(S2[:, :, :, :, :], 0.0).then_inc(cleared, 1)
            pool.memset(red[:, :, :, :], 0.0).then_inc(cleared, 1)
            pool.wait_ge(half_ready, 1)
            pool.wait_ge(prep, 1)
            pool.tensor_tensor(rs[:, :], pv[:, :], mhalf[:, :], ALU.pow).then_inc(prep_pow, 1)
            pool.wait_ge(cst_in, 16)
            pool.wait_ge(cleared, 3)

            def power1(a):
                if a.runs():
                    pool.wait_ge(var1, a.t + 1)
                    wait(pool, acc0_ready, a.t - 1)
                    pool.tensor_tensor(r1[:, a.par:a.par + 1], ve1[:, a.par:a.par + 1], mhalf[:, 0:1],
                                       ALU.pow).then_inc(rstd1, 1)

            def power2(a):
                if not a.runs():
                    return
                pool.wait_ge(var2, a.t + 1)
                wait(pool, diag_ready, a.t - 1)
                wait(pool, rstd2_kept, a.t - 1)
                pool.tensor_tensor(r2p[:, a.par:a.par + 1], ve2[:, a.par:a.par + 1], mhalf[:, 0:1],
                                   ALU.pow).then_inc(rstd2, 1)
                waits_apart(pool, a, (rstd2, a.t + 1), (turned, a.t * 3 - 3))
                pool.tensor_scalar(diag[:, a.par, :], cs[:, K_ID:K_ID + P + 2], r2p[:, a.par:a.par + 1], 1.0,
                                   ALU.mult, ALU.mult).then_inc(diag_ready, 1)
                pool.tensor_copy(r2[:, bass.ds(a.t, 1)], r2p[:, a.par:a.par + 1]).then_inc(rstd2_kept, 1)

            def mask_column(a):
                if not a.runs():
                    return
                wait(pool, mask_mix, 8)
                wait(pool, att_done, a.half)
                pool.tensor_copy(red[:, 2, 1:NJ + 1, 2 * a.par:2 * a.par + 2].rearrange("p j b -> p b j"),
                                 mT[:, bass.ds(a.t * 2, 2), :])\
                    .then_inc(mask_col, 1)

            def mask_attention(a):
                if a.par == 0 or not a.runs():
                    return
                pool.wait_ge(sigm, a.half + 1)
                pool.wait_ge(mask_r_in, (a.half + 1) * 16)
                wait(pool, att_stored, a.half * 16)
                pool.tensor_tensor(att_m[:, :], att_s[:, :], mask_r[:, :], ALU.mult).then_inc(att_masked, 1)

            def power3(a):
                if a.runs():
                    pool.wait_ge(var3, a.t + 1)
                    wait(pool, affine3, a.t - 1)
                    pool.tensor_tensor(r3[:, a.par:a.par + 1], ve3[:, a.par:a.par + 1], mhalf[:, 0:1],
                                       ALU.pow).then_inc(rstd3, 1)

            def last_sum(a):
                if a.runs():
                    pool.wait_ge(fin_relu, a.t + 1)
                    pool.tensor_tensor(fin[:, a.par, :], fin[:, a.par, :], X[:, a.t, :], ALU.add)\
                        .then_inc(fin_added, 1)

            def step(h, j):
                mask_attention(Pair(h, j - 5))
                mask_column(Pair(h, j - 4))
                power3(Pair(h, j - 7))
                power1(Pair(h, j))
                last_sum(Pair(h, j - 7))
                power2(Pair(h, j - 3))

            for k in range(FIRST_LOOP):
                step(k // 2, k % 2)
            with pool.Fori(FIRST_LOOP // 2, NT // 2) as h:
                step(h, 0)
                step(h, 1)
            for k in range(NT, STEPS):
                step(k // 2, k % 2)

        @block.scalar
        def _(act):
            act.dma_start(prm[:, :], par).then_inc(par_in, 16)
            act.dma_start(mfull[:, :, :], masks.rearrange("b h w -> h b w")).then_inc(mask_in, 16)
            act.dma_start(selz[:, :, :], sel).then_inc(att_in, 16)
            act.dma_start(atw[:, :], att_w).then_inc(att_in, 16)
            act.wait_ge(w1_in, 16)
            act.activation(w1s[:, :, :].rearrange("p k o -> p (k o)"), w1f, ACT.Sign).then_inc(w1_signs, 1)

            def sign_x(a):
                if not a.runs():
                    return
                wait(act, cleared, 1)
                act.wait_ge(mean1, a.t + 1)
                wait(act, spread[a.par], a.half * 64)
                act.activation(U[:, a.par, PW + 1:PW + 1 + H * PW].rearrange("p (h w) -> p h w", w=PW)[:, :, 0:W],
                               X[:, a.t, :].rearrange("p (h w) -> p h w", w=W), ACT.Sign,
                               bias=nm1[:, a.par:a.par + 1]).then_inc(signed, 1)

            def relu_unit(a, n):
                if not a.runs():
                    return
                act.wait_ge(conv1_done, a.t * 4 + n + 1)
                wait(act, gated, a.t * 4 + n - 3 if n != 3 else a.t * 4)
                q = n % 2
                act.activation(relu[:, n, :].rearrange("p (a n) -> p a n", a=2),
                               big[unit_slot((a.par + SKEW["c1"]) % 2, f"c1_{n}")][:, :, 0:HALF], ACT.Relu,
                               bias=shf[:, q:q + 1], scale=inv[:, q:q + 1]).then_inc(relu_done, 1)

            def start_sum(a):
                if not a.runs():
                    return
                act.wait_ge(bias1, a.t + 1)
                wait(act, y_added, a.t - 1)
                act.activation(acc0[:, a.par, :], X[:, a.t, :], ACT.Identity, bias=b1[:, a.par:a.par + 1],
                               scale=r1[:, a.par:a.par + 1]).then_inc(acc0_ready, 1)

            def sigmoid(a):
                if a.par == 0 or not a.runs():
                    return
                act.wait_ge(att_done, a.half + 1)
                wait(act, att_masked, a.half)
                act.activation(att_s[:, :], small[1][0:4 * NJ, 0:CP], ACT.Sigmoid).then_inc(sigm, 1)

            def last_relu(a):
                if not a.runs():
                    return
                act.wait_ge(affine3, a.t + 1)
                wait(act, stored[a.par], a.half * 16)
                act.activation(fin[:, a.par, :], o[:, a.par, :], ACT.Relu, bias=bi3[:, a.par:a.par + 1],
                               scale=sc3[:, a.par:a.par + 1]).then_inc(fin_relu, 1)

            def step(h, j):
                sigmoid(Pair(h, j - 5))
                relu_unit(Pair(h, j - 1), 0)
                relu_unit(Pair(h, j - 1), 1)
                start_sum(Pair(h, j - 2))
                sign_x(Pair(h, j))
                last_relu(Pair(h, j - 7))
                relu_unit(Pair(h, j - 1), 2)
                relu_unit(Pair(h, j - 1), 3)

            step(0, 0)
            act.wait_ge(w2_in, 16)
            act.activation(w2s[:, :, :, :].rearrange("p q t o -> p (q t o)"), w2f, ACT.Sign).then_inc(w2_signs, 1)
            act.wait_ge(bn1_ready, 1)
            for k in range(1, FIRST_LOOP):
                step(k // 2, k % 2)
            with act.Fori(FIRST_LOOP // 2, NT // 2) as h:
                step(h, 0)
                step(h, 1)
            for k in range(NT, STEPS):
                step(k // 2, k % 2)

        @block.vector
        def _(dve):
            def stats_of(a, n, src, chain, done, mv):
                for i in range(2):
                    dve.bn_stats(bnst[:, n, i, :], src[:, HALF * i:HALF * (i + 1)]).then_inc(chain, 1)
                waits_apart(dve, a, (chain, a.t * 2 + 2))
                dve.bn_aggr(mv[:, a.par, :], bnst[:, n, :, :]).then_inc(done, 1)

            def stats_x(a):
                if not a.runs():
                    return
                waits_apart(dve, a, (x_in[a.par], (a.half + 1) * 16), (local1, a.t), (group1, a.t - 1),
                            (var1, a.t - 1))
                stats_of(a, 0, X[:, a.t, :], stats1, local1, mv1)

            def group_terms(a, mv, nm, ps, group, mean, chain, ve, var):
                dve.wait_ge(group, a.t + 1)
                dve.tensor_scalar(nm, ps[:, 0:1], -1.0, None, ALU.mult).then_inc(mean, 1)
                dve.tensor_scalar(tmp[:, 0:1], ps[:, 1:2], EPS, None, ALU.add).then_inc(chain, 1)
                dve.wait_ge(mean, a.t + 1)
                dve.tensor_tensor(dm[:, 0:1], mv[:, a.par, 0:1], nm, ALU.add).then_inc(chain, 1)
                dve.wait_ge(chain, a.t * 2 + 2)
                dve.scalar_tensor_tensor(ve[:, a.par:a.par + 1], dm[:, 0:1], dm[:, 0:1], tmp[:, 0:1],
                                         ALU.mult, ALU.add).then_inc(var, 1)

            def terms1(a):
                if not a.runs():
                    return
                wait(dve, signed, a.t - 1)
                wait(dve, rstd1, a.t - 1)
                wait(dve, bias1, a.t - 1)
                wait(dve, var1, a.t)
                group_terms(a, mv1, nm1[:, a.par:a.par + 1], small[1], group1, mean1, steps1, ve1, var1)

            def make_bias1(a):
                if not a.runs():
                    return
                dve.wait_ge(rstd1, a.t + 1)
                if a.known and a.t == 0:
                    dve.wait_ge(beta_ready, 1)
                wait(dve, acc0_ready, a.t - 1)
                dve.scalar_tensor_tensor(b1[:, a.par:a.par + 1], nm1[:, a.par:a.par + 1],
                                         r1[:, a.par:a.par + 1], beta[:, :], ALU.mult, ALU.add)\
                   .then_inc(bias1, 1)

            def gate(a, n):
                if not a.runs():
                    return
                dve.wait_ge(relu_done, a.t * 4 + n + 1)
                wait(dve, conv2_done, a.t * 2 - 2)
                i, q = n // 2, n % 2
                dst = S2[:, a.par, i, q, PW + 1:PW + 1 + (H - 1) * PW + W]
                dst = bass.AP(dst.tensor, dst.offset, [list(dst.ap[0]), [PW, H], [1, W]])
                dve.tensor_scalar(dst, relu[:, n, :].rearrange("p (h w) -> p h w", w=W), 0.0, None,
                                  ALU.is_gt).then_inc(gated, 1)

            def split_sums(a, i):
                if not a.runs():
                    return
                dve.wait_ge(conv2_done, a.t * 2 + i + 1)
                wait(dve, y_done, a.t - 1)
                v = big[unit_slot((a.par + SKEW["c2"]) % 2, f"c2_{i}")][:, :, 0:HALF]
                whole = RD[:, a.par, i, 0, :].rearrange("p (a n) -> p a n", a=2)
                dve.tensor_scalar(whole, v, ROUND, ROUND, ALU.add, ALU.subtract).then_inc(rounded, 1)
                dve.wait_ge(rounded, a.t * 2 + i + 1)
                dve.tensor_tensor(RD[:, a.par, i, 1, :].rearrange("p (a n) -> p a n", a=2), whole, v,
                                  ALU.subtract).then_inc(split, 1)

            def finish_block(a):
                if not a.runs():
                    return
                dve.wait_ge(y_done, a.t + 1)
                dve.wait_ge(acc0_ready, a.t + 1)
                wait(dve, x1_ready, a.t)
                y = big[unit_slot((a.par + SKEW["y"]) % 2, "y")][:, :, 0:HALF]
                dve.tensor_tensor(ysum[:, :].rearrange("p (a n) -> p a n", a=2), y,
                                  acc0[:, a.par, :].rearrange("p (a n) -> p a n", a=2), ALU.add)\
                   .then_inc(y_added, 1)
                dve.wait_ge(y_added, a.t + 1)
                dve.scalar_tensor_tensor(X[:, a.t, :], ysum[:, :], 0.0, X[:, a.t, :], ALU.max, ALU.add)\
                   .then_inc(x1_ready, 1)
                waits_apart(dve, a, (x1_ready, a.t + 1), (local2, a.t), (group2, a.t - 1), (var2, a.t - 1))
                stats_of(a, 1, X[:, a.t, :], stats2, local2, mv2)

            def terms2(a):
                if not a.runs():
                    return
                wait(dve, var2, a.t)
                wait(dve, rstd2, a.t - 1)
                group_terms(a, mv2, nm2[:, bass.ds(a.t, 1)], small[0], group2, mean2, steps2, ve2, var2)

            def make_u(a):
                if not a.runs():
                    return
                dve.wait_ge(mask_bc[a.par], (a.half + 1) * 32)
                wait(dve, turned, a.t * 3 - 3)
                dve.scalar_tensor_tensor(u[:, a.par, :], X[:, a.t, :], nm2[:, bass.ds(a.t, 1)],
                                         mask_b[:, a.par, :], ALU.add, ALU.mult).then_inc(u_ready, 1)

            def reduce_chunks(a, n):
                if not a.runs():
                    return
                dve.wait_ge(turned, a.t * 3 + n + 1)
                wait(dve, att_done, a.half)
                j0, nj = 3 * n, min(3, NJ - 3 * n)
                ps = small[n // 2][0:CP, 0:nj * (P + 2)].rearrange("p (j m) -> p j m", m=P + 2)
                dst = [red[:, c, 1 + j0:1 + j0 + nj, 2 * a.par:2 * a.par + 2] for c in range(2)]
                dve.tensor_reduce(dst[1], ps[:, :, 0:P].rearrange("p j (i c) -> p j i c", i=2), AX_X, ALU.max)\
                   .then_inc(maxed, 1)
                dve.tensor_copy(dst[0], ps[:, :, P:P + 2]).then_inc(pooled, 1)

            def attend(a):
                if not a.runs():
                    return
                dve.wait_ge(att_bc[a.par], (a.half + 1) * 32)
                wait(dve, fin_relu, a.t - 1)
                dve.scalar_tensor_tensor(o[:, a.par, :], X[:, a.t, :], nm2[:, bass.ds(a.t, 1)],
                                         att_b[:, a.par, :], ALU.add, ALU.mult).then_inc(o_ready, 1)
                waits_apart(dve, a, (o_ready, a.t + 1))
                stats_of(a, 2, o[:, a.par, :], stats3, steps3, mv3)
                dve.wait_ge(steps3, a.t * 3 + 1)
                dve.wait_ge(rstd2_kept, a.t + 1)
                dve.tensor_scalar(tmp[:, 2:3], mv3[:, a.par, 1:2], r2[:, bass.ds(a.t, 1)], r2[:, bass.ds(a.t, 1)],
                                  ALU.mult, ALU.mult).then_inc(steps3, 1)
                dve.wait_ge(steps3, a.t * 3 + 2)
                dve.tensor_scalar(ve3[:, a.par:a.par + 1], tmp[:, 2:3], EPS, None, ALU.add).then_inc(var3, 1)

            def affine(a):
                if not a.runs():
                    return
                dve.wait_ge(rstd3, a.t + 1)
                dve.tensor_scalar(sc3[:, a.par:a.par + 1], r3[:, a.par:a.par + 1], r2[:, bass.ds(a.t, 1)],
                                  g5[:, 0:1], ALU.mult, ALU.mult).then_inc(steps3, 1)
                dve.wait_ge(steps3, a.t * 3 + 3)
                dve.scalar_tensor_tensor(bi3[:, a.par:a.par + 1], mv3[:, a.par, 0:1], sc3[:, a.par:a.par + 1],
                                         g5[:, 1:2], ALU.mult, ALU.subtract, reverse1=True)\
                   .then_inc(affine3, 1)

            def step(h, j):
                split_sums(Pair(h, j - 3), 1)
                stats_x(Pair(h, j))
                gate(Pair(h, j - 1), 0)
                attend(Pair(h, j - 7))
                gate(Pair(h, j - 1), 1)
                reduce_chunks(Pair(h, j - 4), 0)
                make_bias1(Pair(h, j - 1))
                split_sums(Pair(h, j - 2), 0)
                terms1(Pair(h, j))
                affine(Pair(h, j - 7))
                finish_block(Pair(h, j - 3))
                reduce_chunks(Pair(h, j - 4), 1)
                gate(Pair(h, j - 1), 2)
                gate(Pair(h, j - 1), 3)
                reduce_chunks(Pair(h, j - 4), 2)
                terms2(Pair(h, j - 3))
                make_u(Pair(h, j - 3))

            n_prep = [0]

            def link(ins):
                n_prep[0] += 1
                ins.then_inc(prep, 1)
                dve.wait_ge(prep, n_prep[0])

            def scales():
                dve.wait_ge(par_in, 16)
                link(dve.tensor_scalar(pv[:, :], prm[:, Q_VAR:Q_VAR + 4], EPS, None, ALU.add))
                dve.wait_ge(prep_pow, 1)
                link(dve.tensor_tensor(inv[:, :], prm[:, Q_SCALE:Q_SCALE + 4], rs[:, :], ALU.mult))
                link(dve.tensor_tensor(tmp[:, :], prm[:, Q_MEAN:Q_MEAN + 4], inv[:, :], ALU.mult))
                dve.tensor_tensor(shf[:, :], prm[:, Q_BIAS:Q_BIAS + 4], tmp[:, :], ALU.subtract)\
                   .then_inc(bn1_ready, 1)

            def mix_scales():
                dve.wait_ge(bn1_ready, 1)
                link(dve.tensor_tensor(kap[:, :], shf[:, 2:4], prm[:, Q_LAM:Q_LAM + 2], ALU.mult))
                dve.tensor_tensor(kaps[:, :], kap[:, 0:1], kap[:, 1:2], ALU.add).then_inc(beta_sum, 1)
                link(dve.tensor_tensor(alpha[:, 0:1], inv[:, 3:4], prm[:, Q_LAM + 1:Q_LAM + 2], ALU.mult))
                link(dve.tensor_scalar(alpha[:, 1:2], inv[:, 2:3], prm[:, Q_LAM:Q_LAM + 1], -SHIFT,
                                       ALU.mult, ALU.mult))
                link(dve.tensor_copy(part[:, 0, :], alpha[:, :]))
                link(dve.tensor_tensor(rest[:, 0, :], alpha[:, :], part[:, 0, :], ALU.subtract))
                link(dve.tensor_copy(part[:, 1, :], rest[:, 0, :]))
                link(dve.tensor_tensor(rest[:, 1, :], rest[:, 0, :], part[:, 1, :], ALU.subtract))
                link(dve.tensor_copy(part[:, 2, :], rest[:, 1, :]))
                link(dve.tensor_scalar(g5[:, :], prm[:, Q_GAMMA:Q_GAMMA + 2], SELECTED, None, ALU.mult))

            def mix_weights():
                dve.wait_ge(cst_in, 16)
                for kind in range(2):
                    for n in range(3):
                        dve.tensor_scalar(wa[:, kind, n, :], cs[:, K_SEL:K_SEL + 64],
                                          part[:, n, kind:kind + 1], None, ALU.mult).then_inc(mix_ready, 1)
                dve.wait_ge(beta_sum, 2)
                dve.tensor_copy(beta[:, :], small[0][:, 0:1]).then_inc(beta_ready, 1)

            def scale_w2():
                dve.wait_ge(w2_signs, 1)
                dve.tensor_scalar(w2t[:, :, :, :].rearrange("p q t o -> p (q t o)"),
                                  w2s[:, :, :, :].rearrange("p q t o -> p (q t o)"),
                                  cs[:, K_SCALE:K_SCALE + 1], None, ALU.mult).then_inc(w2_ready, 1)

            def mask_work():
                dve.wait_ge(mask_h, 1)
                dve.tensor_copy(mh[:, :, :].rearrange("p b h -> p (b h)"), small[0][:, 0:MB * H])\
                   .then_inc(mask_hs, 1)
                dve.wait_ge(mask_hw, 1)
                ps = small[1][0:CP, 0:MB * NJ].rearrange("p (b j) -> p b j", j=NJ)
                dve.tensor_copy(mhw[:, 1:MB + 1, :], ps).then_inc(mask_hs, 1)
                dve.tensor_copy(mhw[:, 0, :], ps[:, 0, :]).then_inc(mask_hs, 1)
                dve.tensor_copy(mhw[:, MB + 1, :], ps[:, MB - 1, :]).then_inc(mask_hs, 1)
                dve.wait_ge(mask_hs, 4)
                n_r = B // MB
                m_v = mT[:, :, :].rearrange("p (b r) j -> p b r j", r=n_r)
                for r in range(n_r):
                    at = (r + 0.5) / n_r - 0.5
                    lo = 0 if at < 0 else 1
                    hi_w = at + 1 if at < 0 else at
                    dve.tensor_scalar(mlo[:, :, :], mhw[:, lo:lo + MB, :], 1.0 - hi_w, None, ALU.mult)\
                       .then_inc(mask_mix, 1)
                    dve.wait_ge(mask_mix, 2 * r + 1)
                    dve.scalar_tensor_tensor(m_v[:, :, r, :], mhw[:, lo + 1:lo + 1 + MB, :], hi_w, mlo[:, :, :],
                                             ALU.mult, ALU.add).then_inc(mask_mix, 1)
                    dve.wait_ge(mask_mix, 2 * r + 2)

            def keep_mask_rows():
                for g in range(2):
                    dve.wait_ge(mask_turned, g + 1)
                    dve.tensor_copy(mR[:, g, :], small[g][0:CP, 0:CP]).then_inc(mask_rows, 1)

            def band_work():
                dve.wait_ge(band_made, 1)
                n = NCH * 3 * CH
                for i in range(2):
                    dve.tensor_copy(band[:, :, RH * i:RH * (i + 1)],
                                    small[i][0:CP, 0:RH * n].rearrange("p (w c) -> p c w", c=n))\
                       .then_inc(band_ready, 1)

            scales()
            step(0, 0)
            mix_scales()
            mix_weights()
            scale_w2()
            mask_work()
            dve.wait_ge(cleared, 3)
            step(0, 1)
            keep_mask_rows()
            step(1, 0)
            band_work()
            for k in range(3, FIRST_LOOP):
                step(k // 2, k % 2)
            with dve.Fori(FIRST_LOOP // 2, NT // 2) as h:
                step(h, 0)
                step(h, 1)
            for k in range(NT, STEPS):
                step(k // 2, k % 2)

        @block.tensor
        def _(pe):
            def group_stats(a, mv, local, ps, group):
                pe.wait_ge(local, a.t + 1)
                pe.matmul(ps[:, 0:2], cs[:, K_PAIR:K_PAIR + P], mv[:, a.par, :], start=True, stop=True)\
                  .then_inc(group, 1)

            def after_sigmoid(a):
                off = a.step - 5
                b = Pair(a.h, off if off % 2 else off - 1)
                if b.runs():
                    pe.wait_ge(sigm, b.half + 1)

            def stats_x(a):
                if not a.runs():
                    return
                b = Pair(a.h, a.off - 5)
                if b.runs():
                    pe.wait_ge(pooled, b.t * 3 + 3)
                after_sigmoid(a)
                wait(pe, var1, a.t)
                group_stats(a, mv1, local1, small[1], group1)

            def stats_x1(a):
                if not a.runs():
                    return
                b = Pair(a.h, a.off - 1)
                if b.runs():
                    pe.wait_ge(pooled, b.t * 3 + 2)
                group_stats(a, mv2, local2, small[0], group2)

            def free_big(name, h, j):
                known = isinstance(h, int)
                found = unit_before(known, 2 * h + j if known else None, j, name)
                if not found:
                    return
                back, other = found
                kind = other.split("_")[0]
                b = Pair(h, j - back - SKEW[kind])
                if kind == "c1":
                    pe.wait_ge(relu_done, b.t * 4 + int(other[-1]) + 1)
                elif kind == "c2":
                    pe.wait_ge(split, b.t * 2 + int(other[-1]) + 1)
                else:
                    pe.wait_ge(y_added, b.t + 1)

            def window(row0, dy, dx, src):
                at = (row0 + dy) * PW + dx
                return bass.AP(src.tensor, src.offset + at, [list(src.ap[0]), [PW, RH], [1, W]])

            def conv1(h, j, n):
                a = Pair(h, j - SKEW["c1"])
                if not a.runs():
                    return
                free_big(f"c1_{n}", h, j)
                pe.wait_ge(spread[a.par], (a.half + 1) * 64)
                i, q = n // 2, n % 2
                acc = big[unit_slot(j, f"c1_{n}")]
                taps = [(1, 0, 0), (1, 0, 1), (1, 0, 2), (0, 2, 0), (0, 2, 2)]
                for hh in range(2):
                    for s, (copy, dy, dx) in enumerate(taps):
                        mm = pe.matmul(acc[:, hh, 0:HALF], w1s[:, s, q * P:(q + 1) * P],
                                       window(RH * hh, dy, dx, R[:, a.par, i, copy, :]),
                                       start=(s == 0), stop=(s == KS - 1))
                mm.then_inc(conv1_done, 1)

            def conv2(h, j, i, between=lambda: None):
                a = Pair(h, j - SKEW["c2"])
                if not a.runs():
                    between()
                    return
                free_big(f"c2_{i}", h, j)
                pe.wait_ge(gated, a.t * 4 + 2 * i + 2)
                acc = big[unit_slot(j, f"c2_{i}")]
                for hh in range(2):
                    if hh == 1:
                        between()
                    for t in range(9):
                        for q in range(2):
                            mm = pe.matmul(acc[64 * q:64 * q + 64, hh, 0:HALF], w2t[:, q, t, :],
                                           window(RH * hh, t // 3, t % 3, S2[:, a.par, i, q, :]),
                                           start=(t == 0), stop=(t == 8))
                mm.then_inc(conv2_done, 1)

            def mix(h, j):
                a = Pair(h, j - SKEW["y"])
                if not a.runs():
                    return
                free_big("y", h, j)
                pe.wait_ge(split, a.t * 2 + 2)
                acc = big[unit_slot(j, "y")]
                for hh in range(2):
                    for m in range(6):
                        for i in range(2):
                            mm = pe.matmul(acc[64 * i:64 * i + 64, hh, 0:HALF], wa[:, m // 3, m % 3, :],
                                           RD[:, a.par, i, m // 3, HALF * hh:HALF * (hh + 1)],
                                           start=(m == 0), stop=(m == 5))
                mm.then_inc(y_done, 1)

            def turn(a, n):
                if not a.runs():
                    return
                if n == 0:
                    pe.wait_ge(u_ready, a.t + 1)
                    pe.wait_ge(diag_ready, a.t + 1)
                    pe.wait_ge(var2, a.t + 1)
                elif n == 1:
                    pe.wait_ge(pooled, a.t * 3 + 1)
                else:
                    b = Pair(a.h, a.off + 4)
                    if b.runs():
                        pe.wait_ge(var1, b.t + 1)
                    after_sigmoid(a)
                for j in range(3 * n, min(3 * n + 3, NJ)):
                    at = (j - 3 * n) * (P + 2)
                    mm = pe.matmul(small[n // 2][0:CP, at:at + P + 2], u[:, a.par, CP * j:CP * (j + 1)],
                                   diag[:, a.par, :], start=True, stop=True)
                mm.then_inc(turned, 1)

            def attention(a):
                if a.par == 0 or not a.runs():
                    return
                pe.wait_ge(pooled, a.t * 3 + 3)
                pe.wait_ge(mask_col, a.t + 1)
                for m in range(9):
                    c, dj = m // 3, m % 3
                    mm = pe.matmul(small[1][0:4 * NJ, 0:CP], red[:, c, dj:dj + NJ, :].rearrange("p j b -> p (j b)"),
                                   band[:, m * CH:(m + 1) * CH, :].rearrange("p k w -> p (k w)"),
                                   start=(m == 0), stop=(m == 8))
                mm.then_inc(att_done, 1)

            def step(h, j):
                def at(skew):
                    a = Pair(h, j - skew)
                    a.h, a.off, a.step = h, j - skew, j
                    return a
                attention(at(5))
                conv1(h, j, 0)
                conv1(h, j, 1)
                turn(at(4), 0)
                conv2(h, j, 0)
                stats_x(at(0))
                mix(h, j)
                turn(at(4), 1)
                conv1(h, j, 2)
                conv1(h, j, 3)
                turn(at(4), 2)
                conv2(h, j, 1, lambda: stats_x1(at(3)))

            def resize_mask():
                pe.wait_ge(mask_in, 16)
                for b in range(MB):
                    mm = pe.matmul(small[0][:, b * H:(b + 1) * H], mfull[:, b, :], cs[:, K_RH:K_RH + H],
                                   start=True, stop=True)
                mm.then_inc(mask_h, 1)

            def resize_mask_w():
                pe.wait_ge(mask_hs, 1)
                for k in range(CH):
                    mm = pe.matmul(small[1][0:CP, 0:MB * NJ], cs[:, K_RW + CP * k:K_RW + CP * (k + 1)],
                                   mh[:, :, k:H:CH], start=(k == 0), stop=(k == CH - 1))
                mm.then_inc(mask_hw, 1)

            def band_matrices():
                pe.wait_ge(att_in, 32)
                n = NCH * 3 * CH
                for w in range(W):
                    mm = pe.matmul(small[w // RH][0:CP, (w % RH) * n:(w % RH + 1) * n],
                                   selz[:, w, :], atw[:, :], start=True, stop=True)
                mm.then_inc(band_made, 1)

            def turn_mask():
                pe.wait_ge(mask_mix, 8)
                for g in range(2):
                    pe.matmul(small[g][0:CP, 0:CP], mT[:, 16 * g:16 * g + 16, :].rearrange("p b j -> p (b j)"),
                              cs[0:CP, K_ID:K_ID + CP], start=True, stop=True).then_inc(mask_turned, 1)

            pe.wait_ge(cst_in, 16)
            step(0, 0)
            pe.wait_ge(beta_sum, 1)
            pe.matmul(small[0][:, 0:1], cs[:, K_FOLD:K_FOLD + P], kaps[:, :], start=True, stop=True)\
              .then_inc(beta_sum, 1)
            pe.wait_ge(beta_ready, 1)
            resize_mask()
            pe.wait_ge(var1, 1)
            resize_mask_w()
            pe.wait_ge(w1_signs, 1)
            pe.wait_ge(mask_hs, 4)
            step(0, 1)
            pe.wait_ge(var1, 2)
            turn_mask()
            pe.wait_ge(w2_ready, 1)
            pe.wait_ge(mask_rows, 2)
            step(1, 0)
            pe.wait_ge(var1, 3)
            band_matrices()
            pe.wait_ge(band_ready, 2)
            pe.wait_ge(mix_ready, 6)
            for k in range(3, FIRST_LOOP):
                step(k // 2, k % 2)
            with pe.Fori(FIRST_LOOP // 2, NT // 2) as h:
                step(h, 0)
                step(h, 1)
            for k in range(NT, STEPS):
                step(k // 2, k % 2)


def resize_weights(n_in, n_out):
    f = np.float32
    inv = f(1.0) / f(n_out / n_in)
    kernel = max(inv, f(1.0))
    at = (np.arange(n_out, dtype=f) + f(0.5)) * inv - f(0.5)
    w = np.maximum(f(0), f(1) - np.abs(at[None, :] - np.arange(n_in, dtype=f)[:, None]) / kernel)
    return (w / w.sum(axis=0, keepdims=True)).astype(f)


def constants():
    cst = np.zeros((P, K_N), np.float32)
    cst[:, K_ID:K_ID + P] = np.eye(P)
    ch = np.arange(P)
    for i in range(2):
        cst[64 * i:64 * i + 64, K_MEAN + i] = 1.0 / C
    cst[:, K_PAIR:K_PAIR + P] = 0.5 * (ch[:, None] // 2 == ch[None, :] // 2)
    cst[:, K_FOLD:K_FOLD + P] = ch[:, None] % 64 == ch[None, :] % 64
    cst[:, K_SEL:K_SEL + 64] = ch[:, None] % 64 == ch[None, :64]
    cst[:, K_RH:K_RH + H] = resize_weights(MH, H)
    for k in range(CH):
        cst[:, K_RW + CP * k + W * k:K_RW + CP * k + W * (k + 1)] = resize_weights(MW, W)
    cst[:, K_SCALE] = np.where(ch < 64, 1.0 / SHIFT, 1.0)
    sel = np.zeros((CH, KW, W, CH, W), np.float32)
    for k in range(CH):
        for dx in range(KW):
            sel[k, dx, :, k, :] = np.eye(W, k=dx - 3)
    return cst, sel.reshape(CH * KW, W, CP)


def kernel(x, L0_conv_w1, L0_conv_bn1_scale, L0_conv_bn1_bias, L0_conv_bn1_mean, L0_conv_bn1_var, L0_conv_w2,
           L0_conv_bn2_scale, L0_conv_bn2_bias, L0_conv_bn2_mean, L0_conv_bn2_var, L0_conv_lambdas,
           L1_conv_masks, L1_conv_conv_w, L1_conv_in_gamma, L1_conv_in_beta):
    import concourse.bacc as bacc
    from concourse.bass_utils import run_bass_kernel_spmd

    w1 = np.asarray(L0_conv_w1).transpose(1, 2, 3, 0)
    w1_l = np.zeros((2, C, KS, G * 64), np.float32)
    for dx in range(3):
        w1_l[0, :, dx] = w1[:, 0, dx]
        w1_l[1, :, dx] = w1[:, 1, dx]
    w1_l[0, :, 3], w1_l[1, :, 3], w1_l[0, :, 4] = w1[:, 2, 0], w1[:, 2, 1], w1[:, 2, 2]
    w2 = np.asarray(L0_conv_w2).reshape(2, 2, 64, C, 9)
    w2_l = np.ascontiguousarray(w2.transpose(1, 3, 0, 4, 2)).reshape(P, 2 * 9 * 64)
    prm = np.zeros((P, Q_N), np.float32)
    for at, one, two in ((Q_SCALE, L0_conv_bn1_scale, L0_conv_bn2_scale), (Q_BIAS, L0_conv_bn1_bias, L0_conv_bn2_bias),
                         (Q_MEAN, L0_conv_bn1_mean, L0_conv_bn2_mean), (Q_VAR, L0_conv_bn1_var, L0_conv_bn2_var)):
        prm[:, at:at + 2] = np.asarray(one).reshape(2, P).T
        prm[:, at + 2:at + 4] = np.asarray(two).reshape(2, 2, 64).transpose(0, 2, 1).reshape(P, 2)
    prm[:, Q_LAM:Q_LAM + 2] = np.repeat(np.asarray(L0_conv_lambdas).reshape(2, 2), 64, axis=0)
    prm[:, Q_GAMMA] = np.tile(np.asarray(L1_conv_in_gamma), 2)
    prm[:, Q_BETA] = np.tile(np.asarray(L1_conv_in_beta), 2)
    cw = np.asarray(L1_conv_conv_w)[0]
    att = np.zeros((CH, KW, NCH, 3, CH), np.float32)
    for kin in range(CH):
        for dj in range(3):
            for k in range(CH):
                dy = CH * (dj - 1) + kin - k + 3
                if 0 <= dy < KW:
                    att[kin, :, :, dj, k] = cw[:, dy, :].T
    cst, sel = constants()
    arrays = {
        "x": np.asarray(x), "w1": w1_l.reshape(P, KS * G * 64), "w2": w2_l, "par": prm,
        "masks": np.asarray(L1_conv_masks), "att_w": att.reshape(CH * KW, NCH * 3 * CH), "cst": cst, "sel": sel,
    }
    nc = bacc.Bacc("TRN2", target_bir_lowering=False, num_devices=1)
    args = {n: nc.dram_tensor(f"in_{n}", a.shape, mybir.dt.from_np(a.dtype), kind="ExternalInput").ap()
            for n, a in arrays.items()}
    out = nc.dram_tensor("out", (B, C, H, W), F32, kind="ExternalOutput").ap()
    build(nc, *args.values(), out)
    r = run_bass_kernel_spmd(nc, [{f"in_{n}": a for n, a in arrays.items()}], core_ids=[0])
    return r.results[0]["out"]
```
